# Optimizing a Trainium2 kernel written in Bass

```python
import numpy as np
import jax
import jax.numpy as jnp

def _softmax(x, axis=-1):
    return jax.nn.softmax(x, axis=axis)

def _gelu(x):
    return jax.nn.gelu(x, approximate=True)

def _silu(x):
    return jax.nn.silu(x)

def _sigmoid(x):
    return jax.nn.sigmoid(x)

def _layernorm(x, axis=-1, eps=1e-05):
    m = jnp.mean(x, axis=axis, keepdims=True)
    v = jnp.var(x, axis=axis, keepdims=True)
    return (x - m) / jnp.sqrt(v + eps)

def _scatter_add(tgt, idx, src, axis=0):
    return tgt.at[idx].add(src)

def _segment_sum(src, seg, n):
    return jax.ops.segment_sum(src, seg, n)
kernel_name = 'mk_flamingo_gated_d2_seqx_r8_1b5a06'

def setup_inputs(seed: int=0):
    np.random.seed(seed)
    _w = jnp.asarray

    def _rec_inputs():
        import jax
        import jax.numpy as jnp
        _rk = jax.random.key(seed)
        x = 0.0001212 + 1 * jax.random.normal(jax.random.fold_in(_rk, 1), (8, 128, 512), jnp.float32)
        _lenS = 128 - jax.random.randint(jax.random.fold_in(_rk, 7), (8,), 0, max(1, 128 // 4) + 1, jnp.int32)
        _lenS2 = 128 - jax.random.randint(jax.random.fold_in(_rk, 8), (8,), 0, max(1, 128 // 4) + 1, jnp.int32)
        _ctx_4096P = jax.random.normal(jax.random.fold_in(_rk, 11), (8, 16, 512), jnp.float32)
        _ctx_4096c = jax.random.dirichlet(jax.random.fold_in(_rk, 511), 0.3 * jnp.ones((16,), jnp.float32), (8, 128))
        _ctx_4096t = jnp.einsum('bsk,bkd->bsd', _ctx_4096c, _ctx_4096P)
        _ctx_4096t = _ctx_4096t * jax.lax.rsqrt(jnp.mean(jnp.square(_ctx_4096t)) + 1e-12) * 0.953939
        ctx_4096 = -0.000125008 + 0.999885 * (_ctx_4096t + 0.3 * jax.random.normal(jax.random.fold_in(_rk, 611), (8, 128, 512), jnp.float32))
        itok_BxS2_0_2047 = jax.random.randint(jax.random.fold_in(_rk, 12), (8, 128), 0, 256, jnp.int32)
        _g = jax.random.normal(jax.random.fold_in(_rk, 9001), (2, 2), jnp.float32)
        _g = jnp.sign(_g) * jnp.maximum(jnp.abs(_g), 1.0) + (_g == 0) * 1.0
        g_xattn = _g[0]
        g_ffn = _g[1]
        return (x, ctx_4096, itok_BxS2_0_2047, g_xattn, g_ffn)
    x, ctx_4096, itok_BxS2_0_2047, g_xattn, g_ffn = _rec_inputs()

    def _L0_xattn_setup():
        import jax, jax.numpy as jnp
        import numpy as np
        N, C, S = (16, 64, 512)
        rng = jax.random.key(seed)
        k1, k2, k3 = jax.random.split(rng, 3)
        return {'key': jax.random.normal(k1, (N, C, S), dtype=jnp.float32), 'value': jax.random.normal(k2, (N, C, S), dtype=jnp.float32), 'query': jax.random.normal(k3, (N, C, S), dtype=jnp.float32)}
    _L0_xattn_all = _L0_xattn_setup()
    _L0_xattn_in = {k: v for k, v in _L0_xattn_all.items() if k in ()}
    del _L0_xattn_all

    def _L0_ffn_setup():
        import jax, jax.numpy as jnp
        import numpy as np
        B, T, D_IN, D_OUT = (8, 256, 512, 512)
        N_LORAS, RANK = (16, 32)
        SCALING = 1.0
        key = jax.random.key(seed)
        ks = jax.random.split(key, 8)
        std = 1.0 / D_IN ** 0.5
        x = jax.random.normal(ks[0], (B, T, D_IN), dtype=jnp.float32)
        idx = jax.random.randint(ks[1], (B,), 0, N_LORAS)
        gate = jax.nn.one_hot(idx, N_LORAS, dtype=jnp.float32)
        kernel = jax.random.normal(ks[2], (D_IN, D_OUT), dtype=jnp.float32) * std
        bias = jnp.zeros((D_OUT,), dtype=jnp.float32)
        lora_A = jax.random.normal(ks[3], (N_LORAS, RANK, D_IN), dtype=jnp.float32) * std
        lora_B = jax.random.normal(ks[4], (N_LORAS, D_OUT, RANK), dtype=jnp.float32) * 0.01
        lora_A_shared = jax.random.normal(ks[5], (RANK, D_IN), dtype=jnp.float32) * std
        lora_B_shared = jax.random.normal(ks[6], (D_OUT, RANK), dtype=jnp.float32) * 0.01
        return {'x': x, 'gate': gate, 'kernel': kernel, 'bias': bias, 'lora_A': lora_A, 'lora_B': lora_B, 'lora_A_shared': lora_A_shared, 'lora_B_shared': lora_B_shared}
    _L0_ffn_all = _L0_ffn_setup()
    _L0_ffn_in = {k: v for k, v in _L0_ffn_all.items() if k in ('gate', 'kernel', 'bias', 'lora_A', 'lora_B', 'lora_A_shared', 'lora_B_shared')}
    del _L0_ffn_all

    def _L1_xattn_setup():
        import jax, jax.numpy as jnp
        import numpy as np
        HIDDEN = 512
        N_HEADS = 32
        N_KV_HEADS = 8
        HEAD_DIM = HIDDEN // N_HEADS
        N_REP = N_HEADS // N_KV_HEADS
        ROPE_THETA = 10000.0
        B, S = (2, 256)

        def _rotate_half(x):
            x1, x2 = jnp.split(x, 2, axis=-1)
            return jnp.concatenate((-x2, x1), axis=-1)

        def _rope_cos_sin(position_ids):
            inv_freq = 1.0 / ROPE_THETA ** (jnp.arange(0, HEAD_DIM, 2, dtype=jnp.float32) / HEAD_DIM)
            freqs = position_ids[..., None].astype(jnp.float32) * inv_freq
            emb = jnp.concatenate((freqs, freqs), axis=-1)
            return (jnp.cos(emb)[:, None, :, :], jnp.sin(emb)[:, None, :, :])
        key = jax.random.key(seed)
        ks = jax.random.split(key, 9)
        sc = 1.0 / np.sqrt(HIDDEN)
        query = jax.random.normal(ks[0], (B, S, HIDDEN), jnp.float32)
        key_t = jax.random.normal(ks[1], (B, S, HIDDEN), jnp.float32)
        value = jax.random.normal(ks[2], (B, S, HIDDEN), jnp.float32)
        position_ids = jnp.sort(jax.random.randint(ks[3], (B, S), 0, S), axis=-1)
        Wq = jax.random.normal(ks[4], (HIDDEN, N_HEADS * HEAD_DIM), jnp.float32) * sc
        Wk = jax.random.normal(ks[5], (HIDDEN, N_KV_HEADS * HEAD_DIM), jnp.float32) * sc
        Wv = jax.random.normal(ks[6], (HIDDEN, N_KV_HEADS * HEAD_DIM), jnp.float32) * sc
        Wo = jax.random.normal(ks[7], (N_HEADS * HEAD_DIM, HIDDEN), jnp.float32) * sc
        return {'query': query, 'key': key_t, 'value': value, 'position_ids': position_ids, 'Wq': Wq, 'Wk': Wk, 'Wv': Wv, 'Wo': Wo}
    _L1_xattn_all = _L1_xattn_setup()
    _L1_xattn_in = {k: v for k, v in _L1_xattn_all.items() if k in ('Wq', 'Wk', 'Wv', 'Wo')}
    del _L1_xattn_all

    def _L1_ffn_setup():
        import jax, jax.numpy as jnp
        import numpy as np
        MAX_THRESHOLD = 1.0 / 8.0
        SCALING = 32.0 / 16.0
        key = jax.random.key(seed)
        ks = jax.random.split(key, 8)
        B_, S, D, O, E, R = (4, 256, 512, 512, 8, 16)
        sd = 1.0 / np.sqrt(D)
        return {'x': jax.random.normal(ks[0], (B_, S, D), jnp.float32), 'W_base': jax.random.normal(ks[1], (O, D), jnp.float32) * sd, 'b_base': jax.random.normal(ks[2], (O,), jnp.float32) * 0.01, 'W_gate': jax.random.normal(ks[3], (E, D), jnp.float32) * sd, 'W_thr': jax.random.normal(ks[4], (1, D), jnp.float32) * sd, 'b_thr': jax.random.normal(ks[5], (1,), jnp.float32) * 0.01, 'A': jax.random.normal(ks[6], (E, R, D), jnp.float32) * sd, 'B': jax.random.normal(ks[7], (O,), jnp.float32)[None, :, None] * jnp.zeros((E, O, R), jnp.float32) + jax.random.normal(jax.random.fold_in(key, 7), (E, O, R), jnp.float32) * (1.0 / np.sqrt(R))}
    _L1_ffn_all = _L1_ffn_setup()
    _L1_ffn_in = {k: v for k, v in _L1_ffn_all.items() if k in ('W_base', 'b_base', 'W_gate', 'W_thr', 'b_thr', 'A', 'B')}
    del _L1_ffn_all
    return {'x': x, 'ctx_4096': ctx_4096, 'itok_BxS2_0_2047': itok_BxS2_0_2047, 'g_xattn': g_xattn, 'g_ffn': g_ffn, 'L0_ffn_gate': _L0_ffn_in['gate'], 'L0_ffn_kernel': _L0_ffn_in['kernel'], 'L0_ffn_bias': _L0_ffn_in['bias'], 'L0_ffn_lora_A': _L0_ffn_in['lora_A'], 'L0_ffn_lora_B': _L0_ffn_in['lora_B'], 'L0_ffn_lora_A_shared': _L0_ffn_in['lora_A_shared'], 'L0_ffn_lora_B_shared': _L0_ffn_in['lora_B_shared'], 'L1_xattn_Wq': _L1_xattn_in['Wq'], 'L1_xattn_Wk': _L1_xattn_in['Wk'], 'L1_xattn_Wv': _L1_xattn_in['Wv'], 'L1_xattn_Wo': _L1_xattn_in['Wo'], 'L1_ffn_W_base': _L1_ffn_in['W_base'], 'L1_ffn_b_base': _L1_ffn_in['b_base'], 'L1_ffn_W_gate': _L1_ffn_in['W_gate'], 'L1_ffn_W_thr': _L1_ffn_in['W_thr'], 'L1_ffn_b_thr': _L1_ffn_in['b_thr'], 'L1_ffn_A': _L1_ffn_in['A'], 'L1_ffn_B': _L1_ffn_in['B']}

def reference(x, ctx_4096, itok_BxS2_0_2047, g_xattn, g_ffn, L0_ffn_gate, L0_ffn_kernel, L0_ffn_bias, L0_ffn_lora_A, L0_ffn_lora_B, L0_ffn_lora_A_shared, L0_ffn_lora_B_shared, L1_xattn_Wq, L1_xattn_Wk, L1_xattn_Wv, L1_xattn_Wo, L1_ffn_W_base, L1_ffn_b_base, L1_ffn_W_gate, L1_ffn_W_thr, L1_ffn_b_thr, L1_ffn_A, L1_ffn_B):
    import jax
    import jax.numpy as jnp

    def _L0_xattn_ref(key, value, query):
        import jax, jax.numpy as jnp
        import numpy as np
        N, C, S = (16, 64, 512)
        KC = key.shape[1]
        sim = jnp.einsum('ncs,nds->ncd', key, query) * KC ** (-0.5)
        sim = jax.nn.softmax(sim, axis=1)
        context = jnp.einsum('ncd,nds->ncs', sim, value)
        return context

    def _L0_ffn_ref(x, gate, kernel, bias, lora_A, lora_B, lora_A_shared, lora_B_shared):
        import jax, jax.numpy as jnp
        import numpy as np
        B, T, D_IN, D_OUT = (8, 256, 512, 512)
        N_LORAS, RANK = (16, 32)
        SCALING = 1.0
        base_out = jnp.matmul(x, kernel) + bias
        b = gate.shape[0]
        x_flat = x.reshape(b, -1, x.shape[-1])
        A_eff = jnp.einsum('bn,nri->bri', gate, lora_A)
        B_eff = jnp.einsum('bn,nor->bor', gate, lora_B)
        Ax = jnp.einsum('bri,bti->btr', A_eff, x_flat)
        delta_flat = jnp.einsum('bor,btr->bto', B_eff, Ax)
        Ax_s = jnp.einsum('ri,bti->btr', lora_A_shared, x_flat)
        delta_flat = delta_flat + jnp.einsum('or,btr->bto', lora_B_shared, Ax_s)
        delta = delta_flat.reshape(x.shape[:-1] + (kernel.shape[-1],))
        return base_out + (SCALING * delta).astype(base_out.dtype)

    def _L1_xattn_ref(query, key, value, position_ids, Wq, Wk, Wv, Wo):
        import jax, jax.numpy as jnp
        import numpy as np
        HIDDEN = 512
        N_HEADS = 32
        N_KV_HEADS = 8
        HEAD_DIM = HIDDEN // N_HEADS
        N_REP = N_HEADS // N_KV_HEADS
        ROPE_THETA = 10000.0
        B, S = (2, 256)

        def _rotate_half(x):
            x1, x2 = jnp.split(x, 2, axis=-1)
            return jnp.concatenate((-x2, x1), axis=-1)

        def _rope_cos_sin(position_ids):
            inv_freq = 1.0 / ROPE_THETA ** (jnp.arange(0, HEAD_DIM, 2, dtype=jnp.float32) / HEAD_DIM)
            freqs = position_ids[..., None].astype(jnp.float32) * inv_freq
            emb = jnp.concatenate((freqs, freqs), axis=-1)
            return (jnp.cos(emb)[:, None, :, :], jnp.sin(emb)[:, None, :, :])
        nb, q_len, _ = query.shape
        q = jnp.einsum('bse,ef->bsf', query, Wq).reshape(nb, q_len, N_HEADS, HEAD_DIM).transpose(0, 2, 1, 3)
        k = jnp.einsum('bse,ef->bsf', key, Wk).reshape(nb, q_len, N_KV_HEADS, HEAD_DIM).transpose(0, 2, 1, 3)
        v = jnp.einsum('bse,ef->bsf', value, Wv).reshape(nb, q_len, N_KV_HEADS, HEAD_DIM).transpose(0, 2, 1, 3)
        cos, sin = _rope_cos_sin(position_ids)
        q = q * cos + _rotate_half(q) * sin
        k = k * cos + _rotate_half(k) * sin
        k = jnp.repeat(k, N_REP, axis=1)
        v = jnp.repeat(v, N_REP, axis=1)
        scale = 1.0 / jnp.sqrt(jnp.asarray(HEAD_DIM, q.dtype))
        scores = jnp.einsum('bhqd,bhkd->bhqk', q, k) * scale
        probs = jax.nn.softmax(scores, axis=-1)
        ctx = jnp.einsum('bhqk,bhkd->bhqd', probs, v)
        ctx = ctx.transpose(0, 2, 1, 3).reshape(nb, q_len, N_HEADS * HEAD_DIM)
        return jnp.einsum('bsf,fe->bse', ctx, Wo)

    def _L1_ffn_ref(x, W_base, b_base, W_gate, W_thr, b_thr, A, B):
        import jax, jax.numpy as jnp
        import numpy as np
        MAX_THRESHOLD = 1.0 / 8.0
        SCALING = 32.0 / 16.0
        base = jnp.einsum('bsd,od->bso', x, W_base) + b_base
        D = x.shape[-1]
        xf = x.reshape(-1, D)
        gate_logits = jax.nn.softmax(xf @ W_gate.T, axis=-1)
        thresholds = jax.nn.sigmoid(xf @ W_thr.T + b_thr) * MAX_THRESHOLD
        adapted = gate_logits - thresholds
        selected = (adapted >= 0).astype(x.dtype)
        weights = adapted * selected
        wsum = jnp.sum(weights, axis=-1, keepdims=True)
        wsum = jnp.where(wsum == 0, jnp.ones_like(wsum), wsum)
        weights = weights / wsum
        h = jnp.einsum('nd,erd->ner', xf, A)
        moe = jnp.einsum('ner,ne,eor->no', h, weights, B) * SCALING
        out = base + moe.reshape(base.shape)
        return out
    x = x + jnp.tanh(g_xattn[0]) * _L0_xattn_ref(ctx_4096, ctx_4096, _layernorm(x, axis=-1))
    x = x + jnp.tanh(g_ffn[0]) * _L0_ffn_ref(_layernorm(x, axis=-1), L0_ffn_gate, L0_ffn_kernel, L0_ffn_bias, L0_ffn_lora_A, L0_ffn_lora_B, L0_ffn_lora_A_shared, L0_ffn_lora_B_shared)
    x = x + jnp.tanh(g_xattn[1]) * _L1_xattn_ref(_layernorm(x, axis=-1), ctx_4096, ctx_4096, itok_BxS2_0_2047, L1_xattn_Wq, L1_xattn_Wk, L1_xattn_Wv, L1_xattn_Wo)
    x = x + jnp.tanh(g_ffn[1]) * _L1_ffn_ref(_layernorm(x, axis=-1), L1_ffn_W_base, L1_ffn_b_base, L1_ffn_W_gate, L1_ffn_W_thr, L1_ffn_b_thr, L1_ffn_A, L1_ffn_B)
    return x

_drawn_inputs = setup_inputs


def setup_inputs(seed=0):
    import zlib

    import numpy as np

    out = dict(_drawn_inputs(seed))
    spreads = {'g_ffn': (-1.0, 0.2), 'L0_ffn_bias': (0.0, 0.1)}
    factors = {'L1_ffn_b_base': 8.0}
    for name, (base, spread) in spreads.items():
        noise = np.random.default_rng([zlib.crc32(name.encode()), seed]).standard_normal(out[name].shape)
        drawn = base * np.exp(spread * noise) if base else spread * noise
        out[name] = jnp.asarray(drawn.astype(out[name].dtype))
    for name, factor in factors.items():
        out[name] = (out[name] * factor).astype(out[name].dtype)
    return out
```

```python
from contextlib import ExitStack

import concourse.bass as bass
import numpy as np
from concourse import mybir

ALU = mybir.AluOpType
ACT = mybir.ActivationFunctionType
AX = mybir.AxisListType
F32 = mybir.dt.float32
F32R = mybir.dt.float32r
I32 = mybir.dt.int32

P = 128
B = 8
D = 512
KC = D // P
SLOTS = 4
GROUPS = B // SLOTS
NL, R0 = 16, 32
H, G, DH = 32, 8, 16
REP = H // G
E, R1 = 8, 16
ER = E * R1
HGW = ER + E + 2
EPS = 1e-5
ROPE_THETA = 10000.0
BANKS = 8


class PsumRing:

    def __init__(self, setup, loop):
        self.place, self.before, seen, last = {}, {}, [0] * BANKS, [None] * BANKS
        for n, name in enumerate(setup):
            self.place[name] = (n % BANKS, seen[n % BANKS], False)
            self.before[name] = last[n % BANKS]
            seen[n % BANKS] += 1
            last[n % BANKS] = name
        self.end_of_setup = list(last)
        before = list(seen)
        last = [None] * BANKS
        for n, name in enumerate(loop):
            b = (len(setup) + n) % BANKS
            if name[0] == "UNUSED":
                continue
            self.place[name] = (b, seen[b], True)
            self.before[name] = last[b]
            seen[b] += 1
            last[b] = name
        self.end_of_loop = list(last)
        self.per = [a - b for a, b in zip(seen, before)]

    def bank(self, name):
        return self.place[name][0]

    def nth(self, name, it):
        b, n, in_loop = self.place[name]
        return it * self.per[b] + n if in_loop else n


def setup_uses():
    u = [("GREP",), ("LBT", 0), ("LBT", 1), ("LBT", 2), ("LBT", 3)]
    u += [("AEFF", c) for c in range(KC)] + [("BEFF", h) for h in range(GROUPS)]
    u += [("AST",), ("BST",)] + [("AGT", c) for c in range(KC)] + [("MBT",)] + [("WBT", c) for c in range(KC)]
    return u


def loop_uses():
    u = [("CT", s) for s in range(SLOTS)]
    for s in range(SLOTS + 1):
        if s < SLOTS:
            u.append(("XT0", s))
        if s:
            u.append(("SIM", s - 1))
    for s in range(SLOTS):
        u += [("CTX0", s), ("KV", s)]
    for p in range(SLOTS // 2):
        u += [("XT1", 2 * p), ("XT1", 2 * p + 1), ("AX", p), ("FFN0", 2 * p), ("FFN0", 2 * p + 1)]
    u += [("XT2", 0), ("Q", 0)]
    for s in range(SLOTS + 1):
        if s < SLOTS:
            u += [("KT", s), ("QN", s)] + [("QT", s, gp) for gp in range(G // 2)]
        if s:
            u.append(("MT", s - 1))
        for g in range(G):
            if s:
                u.append(("S2", s - 1, g))
            if s < SLOTS:
                u.append(("S1", s, g))
            if s and g == 5:
                u.append(("PV", s - 1, 0))
        if s + 1 < SLOTS:
            u.append(("XT2", s + 1))
        if s:
            u.append(("PV", s - 1, 1))
        if s + 1 < SLOTS:
            u.append(("Q", s + 1))
        if s:
            u += [("UT", s - 1, 0), ("UT", s - 1, 1), ("CNT", s - 1), ("WO", s - 1)]
    u.append(("XT3", 0))
    for s in range(SLOTS):
        if s + 1 < SLOTS:
            u.append(("XT3", s + 1))
        u += [("HG", s)] + [("UNUSED", 0)] * (s == 3) + [("BASE", s)]
    u += [("HWT", 0), ("UNUSED", 0), ("HWT", 1), ("HWT", 2), ("UNUSED", 0), ("HWT", 3)]
    return u + [("UNUSED", n) for n in range(-len(u) % BANKS)]


HT_ORDER = ([("XT1", s) for s in range(SLOTS)] + [("XT2", 0), ("XT2", 1), ("XT2", 2), ("CNT", 0), ("XT2", 3)]
            + [("CNT", s) for s in range(1, SLOTS)] + [("XT3", s) for s in range(SLOTS)])


GATE_STEPS = 12


def ht_side(name):
    return (name[1] + (name[0] == "CNT")) % 2


def build(nc, x, ctx, pos, g_xattn, g_ffn, gate, w0, bias0, lora_a, lora_b, lora_as, lora_bs,
          wq, wk, wv, wo, w_base, b_base, w_gate, w_thr, b_thr, moe_a, moe_b, out):
    ring = PsumRing(setup_uses(), loop_uses())
    with ExitStack() as stack:
        def sb(name, shape, dt=F32):
            return stack.enter_context(nc.sbuf_tensor(name, [P] + shape, dt))

        def sem(name):
            return stack.enter_context(nc.semaphore(name))

        stack.enter_context(nc.allow_non_contiguous_dma(reason="small tables and LoRA factors"))

        ident = sb("ident", [P])
        mask_r = sb("mask_r", [R0])
        mask_g = sb("mask_g", [2])
        pick_g = sb("pick_g", [G], F32R)
        gate_t = sb("gate_t", [B])
        gate_rep = sb("gate_rep", [KC, B])
        tg = sb("tg", [4])
        bthr = sb("bthr", [1])
        half_neg = sb("half_neg", [1])
        eps_t = sb("eps_t", [1])
        wait_spot = sb("wait_spot", [1])
        gbias = sb("gbias", [2, D])
        pos_i = sb("pos_i", [B], I32)
        pos_f = sb("pos_f", [B])
        inv_f = sb("inv_f", [DH // 2])
        ang = sb("ang", [B, DH // 2])
        turns = sb("turns", [B, DH // 2])
        rope_cos = sb("rope_cos", [B, DH // 2])
        rope_sin = sb("rope_sin", [B, 2, DH // 2])

        w0_s = sb("w0_s", [2, KC, D], F32R)
        wq_s = sb("wq_s", [2, KC, D], F32R)
        wo_s = sb("wo_s", [2, KC, D], F32R)
        wb_s = sb("wb_s", [2, KC, D], F32R)
        mb_s = sb("mb_s", [2, D], F32R)
        ag_s = sb("ag_s", [2, KC, HGW], F32R)
        wkv = sb("wkv", [KC, 2 * G * DH])
        a_eff = sb("a_eff", [KC, B, R0])
        b_eff = sb("b_eff", [GROUPS, D])
        a_cat = sb("a_cat", [2, KC, 4, R0], F32R)
        b_cat = sb("b_cat", [2, D], F32R)
        b_raw = sb("b_raw", [D])

        X = sb("X", [SLOTS, D])
        XB = sb("XB", [SLOTS, D])
        C = sb("C", [SLOTS, D])
        V1 = sb("V1", [SLOTS, G, 32])
        KO = sb("KO", [SLOTS, G * DH])
        XN = sb("XN", [2, D])
        HT = sb("HT", [2, KC, 2, P], F32R)
        KT1 = sb("KT1", [2, 2, G * DH])
        KS = sb("KS", [G // 2, 2, 2, 32])
        QN = sb("QN", [2, REP * P], F32R)
        sel_q = sb("sel_q", [G // 2, 6, 32], F32R)
        PR = sb("PR", [SLOTS, P])
        QT = sb("QT", [2, G // 2, REP * P], F32R)
        KBD = sb("KBD", [2, G // 2, 2, P], F32R)
        NM = sb("NM", [REP, G])
        NMHL = sb("NMHL", [REP, 2 * G])
        MT = sb("MT", [REP * P], F32R)
        PT = sb("PT", [G, REP * P])
        CU = sb("CU", [2, REP * P])
        RS = sb("RS", [2, REP, REP])
        AXT = sb("AXT", [2, 2, P], F32R)
        HWT = sb("HWT", [2, 2, P], F32R)
        stats = sb("stats", [2, 6])
        mv = sb("mv", [2, 2])
        ve = sb("ve", [2, 1])
        rstd = sb("rstd", [2, 1])
        smx = sb("smx", [SLOTS, 4])
        gt = sb("gt", [SLOTS, E + 1])
        gd = sb("gd", [SLOTS, 12])
        gw = sb("gw", [2, SLOTS, E])


        ct = PT[:, 0:SLOTS].rearrange("p s (c t) -> p s c t", c=KC)
        xt0 = CU[:].rearrange("p s (c t) -> p s c t", c=KC)
        qr = XB[:, 2:4]
        QO = XB[:, 1]
        cn = XB[:, 0]
        hgs = PT[:].rearrange("p g n -> p (g n)")[:, 4 * D:4 * D + SLOTS * HGW].rearrange("p (s n) -> p s n", s=SLOTS)
        lora_a_nat, lora_b_t = PT[:, 0:4], PT[:, 4:8]
        lora_b_nat = XB
        w_base_nat, wo_raw = PT[:, 0:4], PT[:, 4:8]
        moe_a_nat, gate_nat, as_nat, moe_b_nat = XB[:, 0], XB[:, 1], XB[:, 2], XB[:, 3]
        bs_nat = PR[:].rearrange("p a (b r) -> p (a b) r", r=R0)[:, 0:KC]
        spread_n = KO
        gsel = V1[:].rearrange("p s g j -> p (s g j)").rearrange("p (k b r) -> p k b r", k=KC, b=B)

        psum = [stack.enter_context(nc.psum_tensor(f"bank{n}", [P, 512], F32)) for n in range(BANKS)]

        filled = [sem(f"filled{n}") for n in range(BANKS)]
        pos_in, gate_in, bias_in, lora_a_in, lora_b_in, w_kv_in, w0_in, wq_in, w_base_in, wo_in, small_in, bs_in = (
            sem(n) for n in ("pos_in", "gate_in", "bias_in", "lora_a_in", "lora_b_in", "w_kv_in", "w0_in", "wq_in",
                             "w_base_in", "wo_in", "small_in", "bs_in"))
        x_in = [sem(f"x_in{s}") for s in range(SLOTS)]
        ctx_in = [sem(f"ctx_in{s}") for s in range(SLOTS)]
        out_stored = [sem(f"out_stored{s}") for s in range(SLOTS)]
        names = ("ident_made", "spread_made", "tables_made", "masks_made", "rope_args", "trig_done", "sin_signed",
                 "gates_done", "gbias_made", "gate_rep_done", "lbt_done", "gsel_made", "aeff_done", "beff_done",
                 "w0_hi", "w0_lo", "wq_hi", "wq_lo", "wo_hi", "wo_lo", "wb_hi", "wb_lo", "ast_hi", "ast_lo",
                 "braw_shared", "agt_hi", "agt_lo", "mbt_hi", "mbt_lo", "v1_ready", "mt_zeroed", "rope_step",
                 "gates_in", "pool_step")
        (ident_made, spread_made, tables_made, masks_made, rope_args, trig_done, sin_signed, gates_done,
         gbias_made, gate_rep_done, lbt_done, gsel_made, aeff_done, beff_done, w0_hi, w0_lo, wq_hi, wq_lo, wo_hi,
         wo_lo, wb_hi, wb_lo, ast_hi, ast_lo, braw_shared, agt_hi, agt_lo, mbt_hi, mbt_lo, v1_ready, mt_zeroed,
         rope_step, gates_in, pool_step) = (sem(n) for n in names)
        ln_stats, ln_var, ln_eps, ln_rstd, xn_ready, resid_done = (
            sem(n) for n in ("ln_stats", "ln_var", "ln_eps", "ln_rstd", "xn_ready", "resid_done"))
        ct_ready, xt0_ready, max0_ready, exp0_done, sum0_inv, p0_ready = (
            sem(n) for n in ("ct_ready", "xt0_ready", "max0_ready", "exp0_done", "sum0_inv", "p0_ready"))
        ht_hi, ht_lo, acat_hi, acat_lo, braw_ready, bcat_hi, bcat_lo, axt_hi, axt_lo, xb_ready = (
            sem(n) for n in ("ht_hi", "ht_lo", "acat_hi", "acat_lo", "braw_ready", "bcat_hi", "bcat_lo", "axt_hi",
                             "axt_lo", "xb_ready"))
        (k_prod, ko_ready, v_ready, ks_hi, ks_lo, kbd_ready, q_prod, qo_ready, qn_hi, qn_lo, qt_by_act, qt_by_dve,
         max1_done, nm_hi, nm_lo, mt_ready, exp1_done, cu_by_act, cu_by_dve, rs_ready, cn_ready) = (
             sem(n) for n in (
                 "k_prod", "ko_ready", "v_ready", "ks_hi", "ks_lo", "kbd_ready", "q_prod", "qo_ready", "qn_hi",
                 "qn_lo", "qt_by_act", "qt_by_dve", "max1_done", "nm_hi", "nm_lo", "mt_ready", "exp1_done",
                 "cu_by_act", "cu_by_dve", "rs_ready", "cn_ready"))
        hg_ready, base_done, gate_args, gate_exp, gate_step, hw_ready, hwt_hi, hwt_lo, xb3_ready = (
            sem(n) for n in ("hg_ready", "base_done", "gate_args", "gate_exp", "gate_step", "hw_ready", "hwt_hi",
                             "hwt_lo", "xb3_ready"))

        def filled_at(name, it=0):
            return filled[ring.bank(name)], ring.nth(name, it) + 1

        def drained(name, it=0):
            step, s = name[0], (name[1] if len(name) > 1 else 0)
            return {
                "GREP": lambda: (gate_rep_done, 1),
                "LBT": lambda: (lbt_done, s + 1),
                "AEFF": lambda: (aeff_done, s + 1),
                "BEFF": lambda: (beff_done, s + 1),
                "AST": lambda: (ast_lo, 1),
                "BST": lambda: (braw_shared, 2),
                "AGT": lambda: (agt_lo, s + 1),
                "MBT": lambda: (mbt_lo, 1),
                "WBT": lambda: (wb_lo, s + 1),
                "CT": lambda: (ct_ready, slot_n(s, it)),
                "XT0": lambda: (xt0_ready, slot_n(s, it)),
                "SIM": lambda: (exp0_done, slot_n(s, it)),
                "CTX0": lambda: (resid_done, ln_n(0, s, it)),
                "KV": lambda: (v_ready, slot_n(s, it)),
                "XT1": lambda: (ht_lo, ht_n(name, it)),
                "AX": lambda: (axt_lo, pair_n(s, it)),
                "FFN0": lambda: (resid_done, ln_n(1, s, it)),
                "XT2": lambda: (ht_lo, ht_n(name, it)),
                "Q": lambda: (q_prod, 2 * slot_n(s, it)),
                "KT": lambda: (kbd_ready, 2 * slot_n(s, it)),
                "QN": lambda: (qn_lo, slot_n(s, it)),
                "QT": lambda: (qt_by_act if name[2] < 2 else qt_by_dve, it * 2 * SLOTS + (2 * s + name[2] % 2 + 1)),
                "MT": lambda: (mt_ready, slot_n(s, it)),
                "S1": lambda: (max1_done, it * G * SLOTS + (G * s + name[2] + 1)),
                "S2": lambda: (exp1_done, it * G * SLOTS + (G * s + name[2] + 1)),
                "PV": lambda: (cu_by_dve if name[2] else cu_by_act, slot_n(s, it)),
                "UT": lambda: (cn_ready, it * 2 * SLOTS + (2 * s + name[2] + 1)),
                "CNT": lambda: (ht_lo, ht_n(name, it)),
                "WO": lambda: (resid_done, ln_n(2, s, it)),
                "XT3": lambda: (ht_lo, ht_n(name, it)),
                "HG": lambda: (hg_ready, slot_n(s, it)),
                "BASE": lambda: (resid_done, ln_n(3, s, it)),
                "HWT": lambda: (hwt_lo, slot_n(s, it)),
            }[step]()

        def pair_n(p, it):
            return it * (SLOTS // 2) + (p + 1)

        def ln_n(layer, s, it):
            return it * 4 * SLOTS + (layer * SLOTS + s + 1)

        def ht_n(name, it):
            return it * len(HT_ORDER) + (HT_ORDER.index(name) + 1)

        def slot_n(s, it):
            return it * SLOTS + (s + 1)

        block = stack.enter_context(nc.Block())


        @block.sync
        def _(sp):
            lora_b_v = lora_b.rearrange("n (c p) r -> p c n r", p=P)
            lora_b_nat_v = lora_b_nat[:].rearrange("p c (n r) -> p c n r", n=NL)
            w0_v, wq_v = (w.rearrange("(c p) n -> p c n", p=P) for w in (w0, wq))
            for s in range(SLOTS):
                sp.dma_start(X[:, s], x[s]).then_inc(x_in[s], 16)
                sp.dma_start(C[:, s], ctx[s]).then_inc(ctx_in[s], 16)
            sp.dma_start(wkv[:, :, 0:P], wk.rearrange("(c p) n -> p c n", p=P)).then_inc(w_kv_in, 16)
            sp.dma_start(wkv[:, :, P:2 * P], wv.rearrange("(c p) n -> p c n", p=P)).then_inc(w_kv_in, 16)
            sp.dma_start(CU[:], w0_v[:, 0:2]).then_inc(w0_in, 16)
            sp.dma_start(XN[:], w0_v[:, 2:4]).then_inc(w0_in, 16)
            sp.wait_ge(*filled_at(("LBT", KC - 1)))
            sp.dma_start(moe_a_nat, moe_a.rearrange("e r d -> (e r) d")).then_inc(small_in, 16)
            sp.dma_start(gate_nat[0:E], w_gate).then_inc(small_in, 16)
            sp.dma_start(gate_nat[E:E + 1], w_thr).then_inc(small_in, 16)
            sp.dma_start(gate_nat[E + 1:E + 2], w_thr).then_inc(small_in, 16)
            sp.dma_start(as_nat[0:R0], lora_as).then_inc(small_in, 16)
            moe_b_v = moe_b.rearrange("e (c p) r -> p c e r", p=P)
            moe_b_nat_v = moe_b_nat.rearrange("p (c e r) -> p c e r", c=KC, e=E)
            for c in range(KC):
                sp.dma_start(moe_b_nat_v[:, c], moe_b_v[:, c]).then_inc(small_in, 16)
            sp.wait_ge(w0_hi, 2)
            sp.wait_ge(w0_lo, 2)
            sp.dma_start(CU[:], wq_v[:, 0:2]).then_inc(wq_in, 16)
            sp.dma_start(XN[:], wq_v[:, 2:4]).then_inc(wq_in, 16)
            sp.wait_ge(*filled_at(("AEFF", KC - 1)))
            sp.dma_start(w_base_nat, w_base.rearrange("(c p) n -> p c n", p=P)).then_inc(w_base_in, 16)
            sp.wait_ge(*filled_at(("BEFF", GROUPS - 1)))
            sp.dma_start(wo_raw, wo.rearrange("(c p) n -> p c n", p=P)).then_inc(wo_in, 16)

            def store_group(it):
                for s in range(SLOTS):
                    sp.wait_ge(resid_done, ln_n(3, s, it))
                    sp.dma_start(out[it * SLOTS + s], XB[:, s]).then_inc(out_stored[s], 16)

            with sp.Fori(0, GROUPS - 1, 1) as it:
                for s in range(SLOTS):
                    sp.wait_ge(*filled_at(("CTX0", s), it))
                    sp.dma_start(C[:, s], ctx[(it + 1) * SLOTS + s]).then_inc(ctx_in[s], 16)
                for s in range(SLOTS):
                    sp.wait_ge(xb3_ready, slot_n(s, it))
                    sp.wait_ge(xn_ready, ln_n(3, s, it))
                    sp.dma_start(X[:, s], x[(it + 1) * SLOTS + s]).then_inc(x_in[s], 16)
                store_group(it)
            store_group(GROUPS - 1)
            for s in range(SLOTS):
                sp.wait_ge(out_stored[s], 16 * (GROUPS + 1))

        @block.gpsimd
        def _(pool):
            for s in range(SLOTS):
                pool.sem_inc(out_stored[s], 16)
            pool.memset(ident[:], 0.0).then_inc(pool_step, 1)
            pool.memset(spread_n[0:NL], 1.0).then_inc(pool_step, 1)
            pool.wait_ge(pool_step, 1)
            pool.affine_select(out=ident[:], in_=ident[:], compare_op=ALU.not_equal, fill=1.0, base=0,
                               pattern=[[-1, P]], channel_multiplier=1).then_inc(ident_made, 1)
            pool.wait_ge(pool_step, 2)
            pool.affine_select(out=spread_n[0:NL], in_=spread_n[0:NL], compare_op=ALU.is_ge, fill=0.0, base=0,
                               pattern=[[P, KC], [1, P]], channel_multiplier=-R0).then_inc(pool_step, 1)
            pool.wait_ge(pool_step, 3)
            pool.affine_select(out=spread_n[0:NL], in_=spread_n[0:NL], compare_op=ALU.is_ge, fill=0.0, base=R0 - 1,
                               pattern=[[-P, KC], [-1, P]], channel_multiplier=R0).then_inc(spread_made, 1)
            pool.memset(half_neg[:], -0.5).then_inc(tables_made, 1)
            pool.memset(eps_t[:], EPS).then_inc(tables_made, 1)
            for j in range(DH // 2):
                inv = np.float32(1.0) / np.float32(ROPE_THETA) ** np.float32(2 * j / DH)
                pool.memset(inv_f[:, j:j + 1], float(inv)).then_inc(tables_made, 1)
            pool.memset(MT[:].bitcast(F32), 0.0).then_inc(mt_zeroed, 1)
            pool.wait_ge(masks_made, 1)
            pool.wait_ge(gate_rep_done, 1)
            pool.tensor_tensor(gsel, mask_r[:].unsqueeze(1).unsqueeze(1).to_broadcast([P, KC, B, R0]),
                               gate_rep[:].unsqueeze(3).to_broadcast([P, KC, B, R0]), ALU.mult).then_inc(gsel_made, 1)
            pool.wait_ge(gates_done, 1)
            pool.wait_ge(bias_in, 32)
            for layer in range(2):
                pool.tensor_scalar(gbias[:, layer], gbias[:, layer], tg[:, 2 + layer:3 + layer], 0.0, ALU.mult,
                                   ALU.add).then_inc(gbias_made, 1)
            pool.wait_ge(*filled_at(("BEFF", GROUPS - 1)))
            pool.memset(V1[:], 0.0).then_inc(pool_step, 1)
            pool.wait_ge(pool_step, 4)
            pool.memset(V1[:, :, :, DH:DH + 1], 1.0).then_inc(v1_ready, 1)

            def ln_scale(layer, s, it):
                pool.wait_ge(ln_var, ln_n(layer, s, it))
                pool.tensor_tensor(ve[:, s % 2], mv[:, s % 2, 1:2], eps_t[:], ALU.add).then_inc(ln_eps, 1)
                pool.wait_ge(ln_eps, ln_n(layer, s, it))
                pool.tensor_tensor(rstd[:, s % 2], ve[:, s % 2], half_neg[:], ALU.pow).then_inc(ln_rstd, 1)

            def add_bias(layer, s, it):
                if layer == 0:
                    pool.wait_ge(resid_done, ln_n(0, s, it))
                    pool.wait_ge(out_stored[s], 16 * (it + 1))
                else:
                    pool.wait_ge(resid_done, ln_n(2, s, it))
                pool.tensor_tensor(XB[:, s], X[:, s], gbias[:, layer], ALU.add).then_inc(
                    xb3_ready if layer else xb_ready, 1)

            def rotate(dst, a, b, done):
                pool.tensor_tensor(dst[0], a[0], b[1], ALU.add).then_inc(done, 1)
                pool.tensor_tensor(dst[1], a[1], b[0], ALU.add).then_inc(done, 1)

            def k_add(s, it):
                pool.wait_ge(k_prod, 2 * slot_n(s, it))
                a, b = (KT1[:, s % 2, j].rearrange("p (g h d) -> p h g d", g=G, h=2) for j in range(2))
                o = KO[:, s].rearrange("p (g h d) -> p h g d", g=G, h=2)
                rotate([o[:, 0], o[:, 1]], [a[:, 0], a[:, 1]], [b[:, 0], b[:, 1]], ko_ready)

            def k_lo(s, it):
                pool.wait_ge(ks_hi, slot_n(s, it))
                pool.tensor_tensor(KS[:, :, :, 1], KO[:, s].rearrange("p (g n) -> p g n", n=32).unsqueeze(2)
                                   .to_broadcast([P, G // 2, 2, 32]), KS[:, :, :, 0], ALU.subtract).then_inc(ks_lo, 1)

            def q_add(s, it):
                pool.wait_ge(q_prod, 2 * slot_n(s, it))
                a, b = (qr[:, j].rearrange("p (g r h d) -> p h g r d", g=G, r=REP, h=2) for j in range(2))
                o = QO.rearrange("p (r g h d) -> p h g r d", g=G, r=REP, h=2)
                rotate([o[:, 0], o[:, 1]], [a[:, 0], a[:, 1]], [b[:, 0], b[:, 1]], qo_ready)

            with pool.Fori(0, GROUPS, 1) as it:
                for s in range(SLOTS):
                    ln_scale(0, s, it)
                for s in range(SLOTS):
                    ln_scale(1, s, it)
                    k_add(s, it)
                    if s == 0:
                        pool.wait_ge(gbias_made, 2)
                    add_bias(0, s, it)
                for s in range(SLOTS):
                    ln_scale(2, s, it)
                q_add(0, it)
                for s in range(SLOTS + 1):
                    if s < SLOTS:
                        k_lo(s, it)
                    if s >= 2:
                        ln_scale(3, s - 2, it)
                    if s + 1 < SLOTS:
                        q_add(s + 1, it)
                ln_scale(3, SLOTS - 1, it)
                pool.wait_ge(*filled_at(("CNT", SLOTS - 1), it))
                for s in range(SLOTS):
                    add_bias(1, s, it)

        @block.scalar
        def _(act):
            act.dma_start(pos_i[:], pos.rearrange("b t -> t b")).then_inc(pos_in, 16)
            act.dma_start(gate_t[0:NL], gate.rearrange("b n -> n b")).then_inc(gate_in, 16)
            act.dma_start(lora_a_nat, lora_a.rearrange("n r d -> (n r) d").rearrange("(c p) d -> p c d", p=P)).then_inc(
                lora_a_in, 16)
            act.dma_start(tg[:, 0:2], g_xattn.unsqueeze(0).to_broadcast([P, 2])).then_inc(gates_in, 16)
            act.dma_start(tg[:, 2:4], g_ffn.unsqueeze(0).to_broadcast([P, 2])).then_inc(gates_in, 16)
            lora_b_v = lora_b.rearrange("n (c p) r -> p c n r", p=P)
            lora_b_nat_v = lora_b_nat[:].rearrange("p c (n r) -> p c n r", n=NL)
            for c in range(KC):
                act.dma_start(lora_b_nat_v[:, c], lora_b_v[:, c]).then_inc(lora_b_in, 16)
            act.dma_start(bthr[:], b_thr.unsqueeze(0).to_broadcast([P, 1])).then_inc(gates_in, 16)
            act.dma_start(gbias[:, 0], bias0.unsqueeze(0).to_broadcast([P, D])).then_inc(bias_in, 16)
            act.dma_start(gbias[:, 1], b_base.unsqueeze(0).to_broadcast([P, D])).then_inc(bias_in, 16)
            act.dma_start(bs_nat, lora_bs.rearrange("(c p) r -> p c r", p=P)).then_inc(bs_in, 16)

            def copy(out_ap, in_ap):
                return act.activation(out_ap, in_ap, ACT.Copy)

            act.wait_ge(rope_args, 2)
            act.activation(rope_sin[:, :, 0], ang[:], ACT.Sin).then_inc(trig_done, 1)
            act.activation(rope_cos[:], turns[:], ACT.Sin).then_inc(trig_done, 1)
            act.wait_ge(gates_in, 48)
            act.activation(tg[:], tg[:], ACT.Tanh).then_inc(gates_done, 1)
            act.wait_ge(*filled_at(("GREP",)))
            copy(gate_rep[:].rearrange("p k b -> p (k b)"), psum[ring.bank(("GREP",))][:, 0:KC * B]).then_inc(
                gate_rep_done, 1)
            act.wait_ge(w0_in, 32)
            copy(w0_s[:, 0, 0:2], CU[:]).then_inc(w0_hi, 1)
            copy(w0_s[:, 0, 2:4], XN[:]).then_inc(w0_hi, 1)
            for c in range(KC):
                act.wait_ge(*filled_at(("AEFF", c)))
                copy(a_eff[:, c], psum[ring.bank(("AEFF", c))][:, 0:B * R0].rearrange("p (b r) -> p b r", b=B)
                     ).then_inc(aeff_done, 1)
            act.wait_ge(*filled_at(("AST",)))
            shared_a = psum[ring.bank(("AST",))][:, 0:KC * R0].rearrange("p (c r) -> p c r", c=KC).unsqueeze(2)
            copy(a_cat[:, 0, :, 1::2], shared_a.to_broadcast([P, KC, 2, R0])).then_inc(ast_hi, 1)
            for c in range(KC):
                act.wait_ge(*filled_at(("AGT", c)))
                copy(ag_s[:, 0, c], psum[ring.bank(("AGT", c))][:, 0:HGW]).then_inc(agt_hi, 1)
            act.wait_ge(*filled_at(("MBT",)))
            copy(mb_s[:, 0], psum[ring.bank(("MBT",))][:]).then_inc(mbt_hi, 1)
            act.wait_ge(wq_in, 32)
            copy(wq_s[:, 0, 0:2], CU[:]).then_inc(wq_hi, 1)
            copy(wq_s[:, 0, 2:4], XN[:]).then_inc(wq_hi, 1)
            for c in range(KC):
                act.wait_ge(*filled_at(("WBT", c)))
                copy(wb_s[:, 0, c], psum[ring.bank(("WBT", c))][:]).then_inc(wb_hi, 1)
            act.wait_ge(wo_in, 16)
            copy(wo_s[:, 0], wo_raw).then_inc(wo_hi, 1)

            def hi_of_transposed(name, it):
                act.wait_ge(*filled_at(name, it))
                copy(HT[:, 0, :, ht_side(name)], psum[ring.bank(name)][:].rearrange("p (c t) -> p c t", c=KC)
                     ).then_inc(ht_hi, 1)

            def exp0(s, it):
                act.wait_ge(max0_ready, slot_n(s, it))
                act.activation(PR[:, s], psum[ring.bank(("SIM", s))][:, 0:P], ACT.Exp, bias=smx[:, s, 0:1],
                               accum_out=smx[:, s, 1:2]).then_inc(exp0_done, 1)

            def xt0_copy(s, it):
                act.wait_ge(*filled_at(("XT0", s), it))
                act.activation(xt0[:, s % 2], psum[ring.bank(("XT0", s))][:].rearrange("p (c t) -> p c t", c=KC),
                               ACT.Copy, scale=P ** -0.5).then_inc(xt0_ready, 1)

            def a_cat_hi(p, it):
                if p:
                    act.wait_ge(*filled_at(("AX", p - 1), it))
                copy(a_cat[:, 0, :, 0::2], a_eff[:, :, bass.ds(it * SLOTS + 2 * p, 2)]).then_inc(acat_hi, 1)

            def b_cat_hi(p, it):
                act.wait_ge(braw_ready, 2 * pair_n(p, it))
                copy(b_cat[:, 0], b_raw[:]).then_inc(bcat_hi, 1)

            def keys_hi(s, it):
                act.wait_ge(ko_ready, 2 * slot_n(s, it))
                if s:
                    act.wait_ge(*filled_at(("KT", s - 1), it))
                copy(KS[:, :, :, 0].bitcast(F32R), KO[:, s].rearrange("p (g n) -> p g n", n=32).unsqueeze(2)
                     .to_broadcast([P, G // 2, 2, 32])).then_inc(ks_hi, 1)

            with act.Fori(0, GROUPS, 1) as it:
                a_cat_hi(0, it)
                for s in range(SLOTS):
                    act.wait_ge(*filled_at(("CT", s), it))
                    copy(ct[:, s], psum[ring.bank(("CT", s))][:].rearrange("p (c t) -> p c t", c=KC)).then_inc(
                        ct_ready, 1)
                xt0_copy(0, it)
                for s in range(1, SLOTS):
                    xt0_copy(s, it)
                    exp0(s - 1, it)
                exp0(SLOTS - 1, it)
                b_cat_hi(0, it)
                for s in range(SLOTS):
                    act.wait_ge(k_prod, 2 * slot_n(s, it))
                    copy(V1[:, s, :, 0:DH], psum[ring.bank(("KV", s))][:, P:2 * P].rearrange("p (g d) -> p g d", g=G)
                         ).then_inc(v_ready, 1)
                keys_hi(0, it)
                for p in range(SLOTS // 2):
                    hi_of_transposed(("XT1", 2 * p), it)
                    hi_of_transposed(("XT1", 2 * p + 1), it)
                    if p:
                        b_cat_hi(p, it)
                    act.wait_ge(*filled_at(("AX", p), it))
                    copy(AXT[:, 0], psum[ring.bank(("AX", p))][:, 0:2 * P].rearrange("p (s t) -> p s t", s=2)
                         ).then_inc(axt_hi, 1)
                    if p + 1 < SLOTS // 2:
                        a_cat_hi(p + 1, it)
                hi_of_transposed(("XT2", 0), it)
                for s in range(SLOTS + 1):
                    if s < SLOTS:
                        act.wait_ge(*filled_at(("KT", s), it))
                        for g2 in range(2):
                            act.activation(KBD[:, s % 2, :, g2], psum[ring.bank(("KT", s))][:].rearrange(
                                "p (g t) -> p g t", g=G // 2), ACT.Copy, scale=mask_g[:, g2:g2 + 1]).then_inc(
                                kbd_ready, 1)
                        act.wait_ge(*filled_at(("QN", s), it))
                        copy(QN[:, 0], psum[ring.bank(("QN", s))][:]).then_inc(qn_hi, 1)
                        for gp in range(2):
                            act.wait_ge(*filled_at(("QT", s, gp), it))
                            copy(QT[:, s % 2, gp], psum[ring.bank(("QT", s, gp))][:]).then_inc(qt_by_act, 1)
                    if s + 1 < SLOTS:
                        keys_hi(s + 1, it)
                    if s:
                        act.wait_ge(*filled_at(("MT", s - 1), it))
                        copy(MT[0:2 * G], psum[ring.bank(("MT", s - 1))][0:2 * G]).then_inc(mt_ready, 1)
                        for g in range(G):
                            act.wait_ge(*filled_at(("S2", s - 1, g), it))
                            act.activation(PT[:, g], psum[ring.bank(("S2", s - 1, g))][:], ACT.Exp).then_inc(
                                exp1_done, 1)
                    if s + 1 < SLOTS:
                        hi_of_transposed(("XT2", s + 1), it)
                    if s:
                        act.wait_ge(*filled_at(("PV", s - 1, 0), it))
                        copy(CU[:, 0], psum[ring.bank(("PV", s - 1, 0))][:]).then_inc(cu_by_act, 1)
                        hi_of_transposed(("CNT", s - 1), it)
                hi_of_transposed(("XT3", 0), it)
                for s in range(SLOTS):
                    if s + 1 < SLOTS:
                        hi_of_transposed(("XT3", s + 1), it)
                    act.wait_ge(*filled_at(("HG", s), it))
                    copy(hgs[:, s], psum[ring.bank(("HG", s))][:, 0:HGW]).then_inc(hg_ready, 1)
                act.wait_ge(gate_args, it * 2 + 2)
                act.activation(gt[:], gt[:], ACT.Exp).then_inc(gate_exp, 1)
                for s in range(SLOTS):
                    act.wait_ge(*filled_at(("HWT", s), it))
                    copy(HWT[:, s % 2, 0], psum[ring.bank(("HWT", s))][:, 0:P]).then_inc(hwt_hi, 1)

        @block.vector
        def _(dve):
            def recip(out_ap, in_ap):
                return dve.reciprocal(out_ap, in_ap)

            round_up = 1.5 * 2.0 ** 23
            c1, c2 = 6.28125, float(np.float32(2 * np.pi - 6.28125))
            c3 = float(np.float32(2 * np.pi - 6.28125 - c2))
            below_pi = 3.1415925
            step = [0]

            def rope(ins):
                step[0] += 1
                ins.then_inc(rope_step, 1)
                dve.wait_ge(rope_step, step[0])

            dve.wait_ge(ident_made, 1)
            dve.tensor_reduce(mask_r[:], ident[:].rearrange("p (j r) -> p r j", r=R0), AX.X, ALU.add).then_inc(
                masks_made, 1)
            dve.tensor_reduce(mask_g[:], ident[:].rearrange("p (q g d) -> p g q d", g=2, d=DH), AX.XY, ALU.add
                              ).then_inc(masks_made, 1)
            dve.tensor_tensor(pick_g[:], ident[:, 0:G], ident[:, G:2 * G], ALU.add).then_inc(masks_made, 1)
            blocks = ident[:].rearrange("p (g n) -> p g n", n=32).unsqueeze(2).to_broadcast([P, G // 2, 2, 32])
            for first, scale in ((0, DH ** -0.5), (2, 0.0), (4, DH ** -0.5)):
                dve.tensor_scalar(sel_q[:, :, first:first + 2], blocks, scale, None, ALU.mult).then_inc(masks_made, 1)
            dve.wait_ge(tables_made, 2 + DH // 2)
            dve.wait_ge(pos_in, 16)
            rope(dve.tensor_copy(pos_f[:], pos_i[:]))
            rope(dve.tensor_tensor(ang[:], pos_f[:].unsqueeze(2).to_broadcast([P, B, DH // 2]),
                                   inv_f[:].unsqueeze(1).to_broadcast([P, B, DH // 2]), ALU.mult))
            rope(dve.tensor_scalar(turns[:], ang[:], float(1 / (2 * np.pi)), round_up, ALU.mult, ALU.add))
            rope(dve.tensor_scalar(turns[:], turns[:], -round_up, None, ALU.add))
            for c in (c1, c2, c3):
                rope(dve.scalar_tensor_tensor(out=ang[:], in0=turns[:], scalar=-c, in1=ang[:], op0=ALU.mult,
                                              op1=ALU.add))
            rope(dve.tensor_scalar(ang[:], ang[:], below_pi, -below_pi, ALU.min, ALU.max))
            dve.scalar_tensor_tensor(out=turns[:], in0=ang[:], scalar=-1.0, in1=ang[:], op0=ALU.mult, op1=ALU.max
                                     ).then_inc(rope_args, 1)
            dve.wait_ge(rope_args, 1)
            dve.tensor_scalar(turns[:], turns[:], -1.0, float(np.pi / 2), ALU.mult, ALU.add).then_inc(rope_args, 1)
            dve.wait_ge(trig_done, 1)
            dve.tensor_scalar(rope_sin[:, :, 1], rope_sin[:, :, 0], -1.0, None, ALU.mult).then_inc(sin_signed, 1)

            def minus_hi(lo_ap, whole, hi_ap):
                return dve.tensor_tensor(lo_ap, whole, hi_ap.bitcast(F32), ALU.subtract)

            for c in range(KC):
                dve.wait_ge(*filled_at(("LBT", c)))
                dve.tensor_copy(lora_b_t[:, c], psum[ring.bank(("LBT", c))][:]).then_inc(lbt_done, 1)
            dve.wait_ge(w0_hi, 2)
            minus_hi(w0_s[:, 1, 0:2], CU[:], w0_s[:, 0, 0:2]).then_inc(w0_lo, 1)
            minus_hi(w0_s[:, 1, 2:4], XN[:], w0_s[:, 0, 2:4]).then_inc(w0_lo, 1)
            for h in range(GROUPS):
                dve.wait_ge(*filled_at(("BEFF", h)))
                dve.tensor_copy(b_eff[:, h], psum[ring.bank(("BEFF", h))][:]).then_inc(beff_done, 1)
            dve.wait_ge(ast_hi, 1)
            shared_a = psum[ring.bank(("AST",))][:, 0:KC * R0].rearrange("p (c r) -> p c r", c=KC).unsqueeze(2)
            minus_hi(a_cat[:, 1, :, 1::2], shared_a.to_broadcast([P, KC, 2, R0]), a_cat[:, 0, :, 1::2]).then_inc(
                ast_lo, 1)
            dve.wait_ge(*filled_at(("BST",)))
            for j in range(2):
                dve.tensor_copy(b_raw[64 * j + R0:64 * j + 2 * R0], psum[ring.bank(("BST",))][0:R0]).then_inc(
                    braw_shared, 1)
            for c in range(KC):
                dve.wait_ge(agt_hi, c + 1)
                minus_hi(ag_s[:, 1, c], psum[ring.bank(("AGT", c))][:, 0:HGW], ag_s[:, 0, c]).then_inc(agt_lo, 1)
            dve.wait_ge(mbt_hi, 1)
            minus_hi(mb_s[:, 1], psum[ring.bank(("MBT",))][:], mb_s[:, 0]).then_inc(mbt_lo, 1)
            dve.wait_ge(wq_hi, 2)
            minus_hi(wq_s[:, 1, 0:2], CU[:], wq_s[:, 0, 0:2]).then_inc(wq_lo, 1)
            minus_hi(wq_s[:, 1, 2:4], XN[:], wq_s[:, 0, 2:4]).then_inc(wq_lo, 1)
            for c in range(KC):
                dve.wait_ge(wb_hi, c + 1)
                minus_hi(wb_s[:, 1, c], psum[ring.bank(("WBT", c))][:], wb_s[:, 0, c]).then_inc(wb_lo, 1)
            dve.wait_ge(wo_hi, 1)
            minus_hi(wo_s[:, 1], wo_raw, wo_s[:, 0]).then_inc(wo_lo, 1)
            dve.wait_ge(gates_done, 1)
            dve.wait_ge(trig_done, 2)
            dve.wait_ge(sin_signed, 1)
            dve.wait_ge(beff_done, GROUPS)
            dve.wait_ge(braw_shared, 2)

            def ln_moments(layer, s, it):
                if layer == 0:
                    dve.wait_ge(x_in[s], 16 * (it + 1))
                else:
                    dve.wait_ge(resid_done, ln_n(layer - 1, s, it))
                dve.bn_stats(stats[:, s % 2], X[:, s]).then_inc(ln_stats, 1)
                dve.wait_ge(ln_stats, ln_n(layer, s, it))
                dve.memset(wait_spot[:], 0.0)
                dve.bn_aggr(mv[:, s % 2], stats[:, s % 2]).then_inc(ln_var, 1)

            def ln_normalize(layer, s, it):
                dve.wait_ge(ln_rstd, ln_n(layer, s, it))
                if s >= 2:
                    dve.wait_ge(*filled_at((f"XT{layer}", s - 2), it))
                elif layer:
                    dve.wait_ge(*filled_at((f"XT{layer - 1}", s + 2), it))
                dve.tensor_scalar(XN[:, s % 2], X[:, s], mv[:, s % 2, 0:1], rstd[:, s % 2], ALU.subtract,
                                  ALU.mult).then_inc(xn_ready, 1)

            def lo_of_transposed(name, it):
                dve.wait_ge(ht_hi, ht_n(name, it))
                side = ht_side(name)
                minus_hi(HT[:, 1, :, side], psum[ring.bank(name)][:].rearrange("p (c t) -> p c t", c=KC),
                         HT[:, 0, :, side]).then_inc(ht_lo, 1)

            def residual(layer, s, it):
                name = (("CTX0", "FFN0", "WO", "BASE")[layer], s)
                dve.wait_ge(*filled_at(name, it))
                y = psum[ring.bank(name)][:]
                if layer == 0:
                    dve.tensor_tensor(X[:, s], y, X[:, s], ALU.add).then_inc(resid_done, 1)
                elif layer == 2:
                    dve.scalar_tensor_tensor(out=X[:, s], in0=y, scalar=tg[:, 1:2], in1=X[:, s], op0=ALU.mult,
                                             op1=ALU.add).then_inc(resid_done, 1)
                elif layer == 1:
                    dve.wait_ge(xb_ready, slot_n(s, it))
                    dve.scalar_tensor_tensor(out=X[:, s], in0=y, scalar=tg[:, 2:3], in1=XB[:, s], op0=ALU.mult,
                                             op1=ALU.add).then_inc(resid_done, 1)
                else:
                    dve.wait_ge(xb3_ready, slot_n(s, it))
                    dve.scalar_tensor_tensor(out=XB[:, s], in0=y, scalar=tg[:, 3:4], in1=XB[:, s], op0=ALU.mult,
                                             op1=ALU.add).then_inc(resid_done, 1)

            def max0(s, it):
                dve.wait_ge(*filled_at(("SIM", s), it))
                dve.tensor_reduce(smx[:, s, 0:1], psum[ring.bank(("SIM", s))][:, 0:P], AX.X, ALU.max,
                                  negate=True).then_inc(max0_ready, 1)

            def probabilities0(s, it):
                dve.wait_ge(exp0_done, slot_n(s, it))
                recip(smx[:, s, 2:3], smx[:, s, 1:2]).then_inc(sum0_inv, 1)
                dve.wait_ge(sum0_inv, slot_n(s, it))
                dve.tensor_scalar(PR[:, s], PR[:, s], smx[:, s, 2:3], tg[:, 0:1], ALU.mult, ALU.mult).then_inc(
                    p0_ready, 1)

            def a_cat_lo(p, it):
                dve.wait_ge(acat_hi, pair_n(p, it))
                minus_hi(a_cat[:, 1, :, 0::2], a_eff[:, :, bass.ds(it * SLOTS + 2 * p, 2)],
                         a_cat[:, 0, :, 0::2]).then_inc(acat_lo, 1)

            def b_raw_rows(p, it):
                if p:
                    dve.wait_ge(*filled_at(("FFN0", 2 * p - 1), it))
                for j in range(2):
                    r = R0 * (2 * p + j)
                    dve.tensor_copy(b_raw[64 * j:64 * j + R0], b_eff[r:r + R0, bass.ds(it, 1)].squeeze(1)
                                    ).then_inc(braw_ready, 1)

            def b_cat_lo(p, it):
                dve.wait_ge(bcat_hi, pair_n(p, it))
                minus_hi(b_cat[:, 1], b_raw[:], b_cat[:, 0]).then_inc(bcat_lo, 1)

            def axt_lo_part(p, it):
                dve.wait_ge(axt_hi, pair_n(p, it))
                minus_hi(AXT[:, 1], psum[ring.bank(("AX", p))][:, 0:2 * P].rearrange("p (s t) -> p s t", s=2),
                         AXT[:, 0]).then_inc(axt_lo, 1)

            def rotate_products(src, cos_out, sin_out, heads, s, it, done):
                c = rope_cos[:, bass.ds(it * SLOTS + s, 1)].to_broadcast([P, 2 * heads, DH // 2])
                t = rope_sin[:, bass.ds(it * SLOTS + s, 1)].rearrange("p b h d -> p b (h d)").to_broadcast(
                    [P, heads, DH])
                dve.tensor_tensor(cos_out.rearrange("p (h d) -> p h d", d=DH // 2),
                                  src.rearrange("p (h d) -> p h d", d=DH // 2), c, ALU.mult).then_inc(done, 1)
                dve.tensor_tensor(sin_out.rearrange("p (h d) -> p h d", d=DH),
                                  src.rearrange("p (h d) -> p h d", d=DH), t, ALU.mult).then_inc(done, 1)

            def k_products(s, it):
                dve.wait_ge(*filled_at(("KV", s), it))
                if s >= 2:
                    dve.wait_ge(ko_ready, 2 * slot_n(s - 2, it))
                rotate_products(psum[ring.bank(("KV", s))][:, 0:G * DH], KT1[:, s % 2, 0], KT1[:, s % 2, 1], G, s,
                                it, k_prod)

            def q_products(s, it):
                dve.wait_ge(*filled_at(("Q", s), it))
                rotate_products(psum[ring.bank(("Q", s))][:], qr[:, 0], qr[:, 1], H, s, it, q_prod)

            def negative_max(s, it):
                dve.wait_ge(max1_done, it * G * SLOTS + G * (s + 1))
                dve.tensor_copy(NMHL[:, :, 0:G].bitcast(F32R), NM[:]).then_inc(nm_hi, 1)
                dve.wait_ge(nm_hi, slot_n(s, it))
                dve.tensor_tensor(NMHL[:, :, G:2 * G], NM[:], NMHL[:, :, 0:G], ALU.subtract).then_inc(nm_lo, 1)

            def attention_rows(s, half, it):
                name = ("UT", s, half)
                n = it * 2 * SLOTS + (2 * s + half + 1)
                dve.wait_ge(*filled_at(name, it))
                u = psum[ring.bank(name)][:].rearrange("p (r j w) -> p r j w", r=REP, j=REP)
                recip(RS[:, half], u[:, :, :, DH]).then_inc(rs_ready, 1)
                dve.wait_ge(rs_ready, n)
                o = cn[:, half * (D // 2):(half + 1) * (D // 2)].rearrange("p (j r d) -> p r j d", j=REP, r=REP)
                dve.tensor_tensor(o, u[:, :, :, 0:DH], RS[:, half].unsqueeze(3).to_broadcast([P, REP, REP, DH]),
                                  ALU.mult).then_inc(cn_ready, 1)

            with dve.Fori(0, GROUPS, 1) as it:
                a_cat_lo(0, it)
                ln_moments(0, 0, it)
                ln_moments(0, 1, it)
                b_raw_rows(0, it)
                ln_normalize(0, 0, it)
                ln_moments(0, 2, it)
                ln_normalize(0, 1, it)
                ln_moments(0, 3, it)
                max0(0, it)
                ln_normalize(0, 2, it)
                max0(1, it)
                probabilities0(0, it)
                ln_normalize(0, 3, it)
                max0(2, it)
                probabilities0(1, it)
                max0(3, it)
                probabilities0(2, it)
                probabilities0(3, it)
                b_cat_lo(0, it)
                for s in range(SLOTS):
                    residual(0, s, it)
                    ln_moments(1, s, it)
                    k_products(s, it)
                    if s in (1, 2):
                        ln_normalize(1, s - 1, it)
                lo_of_transposed(("XT1", 0), it)
                ln_normalize(1, 2, it)
                lo_of_transposed(("XT1", 1), it)
                ln_normalize(1, 3, it)
                axt_lo_part(0, it)
                a_cat_lo(1, it)
                residual(1, 0, it)
                ln_moments(2, 0, it)
                lo_of_transposed(("XT1", 2), it)
                b_raw_rows(1, it)
                lo_of_transposed(("XT1", 3), it)
                b_cat_lo(1, it)
                axt_lo_part(1, it)
                residual(1, 1, it)
                ln_moments(2, 1, it)
                ln_normalize(2, 0, it)
                ln_normalize(2, 1, it)
                for s in (2, 3):
                    residual(1, s, it)
                    ln_moments(2, s, it)
                lo_of_transposed(("XT2", 0), it)
                ln_normalize(2, 2, it)
                q_products(0, it)
                for s in range(SLOTS + 1):
                    if s < SLOTS:
                        dve.wait_ge(qn_hi, slot_n(s, it))
                        minus_hi(QN[:, 1], psum[ring.bank(("QN", s))][:], QN[:, 0]).then_inc(qn_lo, 1)
                        for gp in range(2, 4):
                            dve.wait_ge(*filled_at(("QT", s, gp), it))
                            dve.tensor_copy(QT[:, s % 2, gp], psum[ring.bank(("QT", s, gp))][:]).then_inc(
                                qt_by_dve, 1)
                    if s >= 2:
                        residual(2, s - 2, it)
                        ln_moments(3, s - 2, it)
                    if s < SLOTS:
                        for g in range(G):
                            gp, m = g // 2, g % 2
                            dve.wait_ge(*filled_at(("S1", s, g), it))
                            dve.tensor_reduce(NM[:, 2 * m:2 * m + 2, 2 * gp:2 * gp + 2],
                                              psum[ring.bank(("S1", s, g))][:].rearrange(
                                                  "p (r g t) -> p r g t", r=2, g=2), AX.X, ALU.max,
                                              negate=True).then_inc(max1_done, 1)
                        negative_max(s, it)
                    if s + 1 < SLOTS:
                        lo_of_transposed(("XT2", s + 1), it)
                    if s == 0:
                        ln_normalize(2, 3, it)
                    if s:
                        dve.wait_ge(*filled_at(("PV", s - 1, 1), it))
                        dve.tensor_copy(CU[:, 1], psum[ring.bank(("PV", s - 1, 1))][:]).then_inc(cu_by_dve, 1)
                    if s + 1 < SLOTS:
                        q_products(s + 1, it)
                    if s:
                        attention_rows(s - 1, 0, it)
                        attention_rows(s - 1, 1, it)
                        lo_of_transposed(("CNT", s - 1), it)
                    if s in (2, 3):
                        ln_normalize(3, s - 2, it)
                residual(2, 3, it)
                ln_moments(3, 3, it)
                lo_of_transposed(("XT3", 0), it)
                ln_normalize(3, 2, it)
                lo_of_transposed(("XT3", 1), it)
                ln_normalize(3, 3, it)
                lo_of_transposed(("XT3", 2), it)
                lo_of_transposed(("XT3", 3), it)

                gates = hgs[:, :, ER:ER + E]
                count = [0]

                def gate_op(ins):
                    count[0] += 1
                    ins.then_inc(gate_step, 1)
                    dve.wait_ge(gate_step, it * GATE_STEPS + count[0])

                dve.wait_ge(hg_ready, slot_n(3, it))
                gate_op(dve.tensor_reduce(gd[:, :, 0], gates, AX.X, ALU.max))
                dve.tensor_tensor(gt[:, :, 0:E], gates, gd[:, :, 0:1].to_broadcast([P, SLOTS, E]),
                                  ALU.subtract).then_inc(gate_args, 1)
                dve.tensor_scalar(gt[:, :, E], hgs[:, :, ER + E], bthr[:], -1.0, ALU.add, ALU.mult).then_inc(
                    gate_args, 1)
                dve.wait_ge(gate_exp, it + 1)
                gate_op(dve.tensor_reduce(gd[:, :, 1], gt[:, :, 0:E], AX.X, ALU.add))
                gate_op(dve.tensor_scalar(gd[:, :, 2], gt[:, :, E], 1.0, None, ALU.add))
                gate_op(recip(gd[:, :, 3:5], gd[:, :, 1:3]))
                gate_op(dve.tensor_tensor(gw[:, 0], gt[:, :, 0:E], gd[:, :, 3:4].to_broadcast([P, SLOTS, E]),
                                          ALU.mult))
                gate_op(dve.scalar_tensor_tensor(out=gw[:, 0], in0=gd[:, :, 4:5].to_broadcast([P, SLOTS, E]),
                                                 scalar=-1.0 / 8.0, in1=gw[:, 0], op0=ALU.mult, op1=ALU.add))
                gate_op(dve.tensor_scalar(gw[:, 0], gw[:, 0], 0.0, None, ALU.max))
                gate_op(dve.tensor_reduce(gd[:, :, 5], gw[:, 0], AX.X, ALU.add))
                gate_op(dve.tensor_scalar(gd[:, :, 6], gd[:, :, 5], 0.0, None, ALU.is_equal))
                gate_op(dve.tensor_tensor(gd[:, :, 7], gd[:, :, 5], gd[:, :, 6], ALU.add))
                gate_op(recip(gd[:, :, 8], gd[:, :, 7]))
                gate_op(dve.scalar_tensor_tensor(out=gw[:, 1], in0=gw[:, 0], scalar=32.0 / 16.0,
                                                 in1=gd[:, :, 8:9].to_broadcast([P, SLOTS, E]), op0=ALU.mult,
                                                 op1=ALU.mult))
                assert count[0] == GATE_STEPS
                for s in range(SLOTS):
                    h = hgs[:, s, 0:ER].rearrange("p (e r) -> p e r", e=E)
                    dve.tensor_tensor(h, h, gw[:, 1, s].unsqueeze(2).to_broadcast([P, E, R1]), ALU.mult).then_inc(
                        hw_ready, 1)
                for s in range(SLOTS):
                    dve.wait_ge(hwt_hi, slot_n(s, it))
                    minus_hi(HWT[:, s % 2, 1], psum[ring.bank(("HWT", s))][:, 0:P], HWT[:, s % 2, 0]).then_inc(
                        hwt_lo, 1)
                    if s:
                        residual(3, s - 1, it)
                residual(3, 3, it)

        @block.tensor
        def _(pe):
            def wait_each(waits, it):
                first, now = waits(0), waits(it)
                for n, (signal, value) in enumerate(first):
                    others = [(v, m) for m, (sg, v) in enumerate(first) if sg is signal and m != n]
                    if all((value, n) > other for other in others):
                        pe.wait_ge(*now[n])

            def take(name, it=0, data=lambda it: []):
                before = ring.before[name]
                wait_each(lambda it: ([drained(before, it)] if before is not None else []) + data(it), it)
                return psum[ring.bank(name)]

            def transposes(name, pieces, it=0, data=lambda it: []):
                bank, col = take(name, it, data), 0
                for n, piece in enumerate(pieces):
                    k, m = piece.shape[0], piece.shape[1]
                    last = pe.transpose(bank[0:m, col:col + k], piece, ident[0:k, 0:k])
                    col += k
                last.then_inc(filled[ring.bank(name)], 1)

            def split_products(bank_ap, x_hl, w_hl, chunks, first=True, last=True):
                n = 0
                for c in range(chunks):
                    for i, j in ((0, 0), (1, 0), (0, 1)):
                        mm = pe.matmul(bank_ap, x_hl(i, c), w_hl(j, c), start=(first and n == 0),
                                       stop=(last and n == 3 * chunks - 1))
                        n += 1
                return mm

            pe.wait_ge(gate_in, 16)
            pe.wait_ge(spread_made, 1)
            bank = take(("GREP",))
            for k in range(KC):
                mm = pe.matmul(bank[:, k * B:(k + 1) * B], spread_n[0:NL, k], gate_t[0:NL], start=(k == 0),
                               stop=(k == KC - 1), skip_group_check=True)
            mm.then_inc(filled[ring.bank(("GREP",))], 1)
            pe.wait_ge(ident_made, 1)
            pe.wait_ge(lora_b_in, 16 * KC)
            for k in range(KC):
                transposes(("LBT", k), [lora_b_nat[:, c, k * P:(k + 1) * P] for c in range(KC)])
            pe.wait_ge(lora_a_in, 16)
            pe.wait_ge(gsel_made, 1)
            for c in range(KC):
                bank = take(("AEFF", c))
                for k in range(KC):
                    mm = pe.matmul(bank[:, 0:B * R0], lora_a_nat[:, k, c * P:(c + 1) * P],
                                   gsel[:, k].rearrange("p b r -> p (b r)"), start=(k == 0), stop=(k == KC - 1))
                mm.then_inc(filled[ring.bank(("AEFF", c))], 1)
            pe.wait_ge(lbt_done, KC)
            for h in range(GROUPS):
                bank = take(("BEFF", h))
                for k in range(KC):
                    mm = pe.matmul(bank[:], gsel[:, k, h * SLOTS:(h + 1) * SLOTS].rearrange("p b r -> p (b r)"),
                                   lora_b_t[:, k], start=(k == 0), stop=(k == KC - 1))
                mm.then_inc(filled[ring.bank(("BEFF", h))], 1)
            pe.wait_ge(small_in, 16 * (5 + KC))
            pe.wait_ge(bs_in, 16)
            transposes(("AST",), [as_nat[0:R0, c * P:(c + 1) * P] for c in range(KC)])
            transposes(("BST",), [bs_nat[:, c] for c in range(KC)])
            for c in range(KC):
                transposes(("AGT", c), [moe_a_nat[:, c * P:(c + 1) * P], gate_nat[0:E + 2, c * P:(c + 1) * P]])
            transposes(("MBT",), [moe_b_nat[:, c * P:(c + 1) * P] for c in range(KC)])
            pe.wait_ge(w_base_in, 16)
            for c in range(KC):
                transposes(("WBT", c), [w_base_nat[:, o, c * P:(c + 1) * P] for o in range(KC)])
            pe.wait_ge(w_kv_in, 32)
            pe.wait_ge(v1_ready, 1)
            pe.wait_ge(mt_zeroed, 1)
            pe.wait_ge(masks_made, 6)
            for done, parts in ((w0_lo, 2), (wq_lo, 2), (agt_lo, KC), (mbt_lo, 1), (wo_lo, 1)):
                pe.wait_ge(done, parts)
            wait_each(lambda it: [drained(name) for name in ring.end_of_setup], 0)

            def contexts(s, it):
                pe.wait_ge(ctx_in[s], 16 * (it + 1))
                transposes(("CT", s), [C[:, s, c * P:(c + 1) * P] for c in range(KC)], it)

            def normalized(layer, s, it):
                pe.wait_ge(xn_ready, ln_n(layer, s, it))
                transposes((f"XT{layer}", s), [XN[:, s % 2, c * P:(c + 1) * P] for c in range(KC)], it)

            def scores0(s, it):
                bank = take(("SIM", s), it, lambda it: [(ct_ready, slot_n(s, it)), (xt0_ready, slot_n(s, it))])
                for c in range(KC):
                    mm = pe.matmul(bank[:, 0:P], xt0[:, s % 2, c], ct[:, s, c], start=(c == 0), stop=(c == KC - 1))
                mm.then_inc(filled[ring.bank(("SIM", s))], 1)

            def context0(s, it):
                pe.wait_ge(p0_ready, slot_n(s, it))
                pe.matmul(take(("CTX0", s), it)[:], PR[:, s], C[:, s], start=True, stop=True).then_inc(
                    filled[ring.bank(("CTX0", s))], 1)

            def keys_values(s, it):
                bank = take(("KV", s), it)
                for c in range(KC):
                    mm = pe.matmul(bank[:, 0:2 * P], ct[:, s, c], wkv[:, c], start=(c == 0), stop=(c == KC - 1))
                mm.then_inc(filled[ring.bank(("KV", s))], 1)

            def lora_down(p, it):
                pe.wait_ge(acat_lo, pair_n(p, it))
                pe.wait_ge(ht_lo, ht_n(("XT1", 2 * p + 1), it))
                bank = take(("AX", p), it)
                split_products(bank[:, 0:2 * P], lambda i, c: a_cat[:, i, c].rearrange("p b r -> p (b r)"),
                               lambda j, c: HT[:, j, c].rearrange("p s t -> p (s t)"), KC).then_inc(
                    filled[ring.bank(("AX", p))], 1)

            def ffn0(s, it):
                bank, half = take(("FFN0", s), it), slice(64 * (s % 2), 64 * (s % 2) + 64)
                split_products(bank[:], lambda i, c: HT[:, i, c, s % 2], lambda j, c: w0_s[:, j, c], KC, last=False)
                pe.wait_ge(axt_lo, pair_n(s // 2, it))
                pe.wait_ge(bcat_lo, pair_n(s // 2, it))
                split_products(bank[:], lambda i, c: AXT[half, i, s % 2], lambda j, c: b_cat[half, j], 1,
                               first=False).then_inc(filled[ring.bank(("FFN0", s))], 1)

            def queries(s, it):
                pe.wait_ge(ht_lo, ht_n(("XT2", s), it))
                bank = take(("Q", s), it)
                split_products(bank[:], lambda i, c: HT[:, i, c, s % 2], lambda j, c: wq_s[:, j, c], KC).then_inc(
                    filled[ring.bank(("Q", s))], 1)

            def keys_on_rows(s, it):
                pe.wait_ge(ks_lo, slot_n(s, it))
                transposes(("KT", s), [KS[:, gp].rearrange("p a b n -> p (a b n)") for gp in range(G // 2)], it)

            def queries_on_rows(s, it):
                pe.wait_ge(qo_ready, 2 * slot_n(s, it))
                transposes(("QN", s), [QO[:, r * P:(r + 1) * P] for r in range(REP)], it)
                for gp in range(G // 2):
                    bank = take(("QT", s, gp), it)
                    sel = sel_q[:, gp].rearrange("p b n -> p (b n)")
                    if gp == 0:
                        pe.wait_ge(qn_lo, slot_n(s, it))
                    pe.matmul(bank[:], sel[:, 0:P], QN[:, 0], start=True, stop=False)
                    pe.matmul(bank[:], sel[:, 64:64 + P], QN[:, 1], start=False, stop=True).then_inc(
                        filled[ring.bank(("QT", s, gp))], 1)

            def scores_for_max(s, g, it):
                gp, m = g // 2, g % 2
                bank = take(("S1", s, g), it, lambda it: [(kbd_ready, 2 * slot_n(s, it)), drained(("QT", s, gp), it)])
                for r in range(2):
                    col = (2 * m + r) * P
                    mm = pe.matmul(bank[:, r * 2 * P:(r + 1) * 2 * P], QT[:, s % 2, gp, col:col + P],
                                   KBD[:, s % 2, gp].rearrange("p g t -> p (g t)"), start=(r == 0), stop=(r == 1),
                                   skip_group_check=True)
                mm.then_inc(filled[ring.bank(("S1", s, g))], 1)

            def max_on_rows(s, it):
                pe.wait_ge(nm_lo, slot_n(s, it))
                bank = take(("MT", s), it)
                for r in range(REP):
                    mm = pe.transpose(bank[0:2 * G, r * P:(r + 1) * P], NMHL[:, r], ident[:])
                mm.then_inc(filled[ring.bank(("MT", s))], 1)

            def scores_less_max(s, g, it):
                bank = take(("S2", s, g), it, lambda it: [(mt_ready, slot_n(s, it))])
                pe.matmul(bank[:], KBD[:, s % 2, g // 2, g % 2], QT[:, s % 2, g // 2], start=True, stop=False)
                pe.matmul(bank[:], pick_g[:, g:g + 1].to_broadcast([P, P]), MT[:], start=False, stop=True).then_inc(
                    filled[ring.bank(("S2", s, g))], 1)

            def values(s, half, it):
                bank = take(("PV", s, half), it, lambda it: [
                    (v_ready, slot_n(s, it)), (exp1_done, it * G * SLOTS + (G * s + 4 * (half + 1)))])
                for j in range(4):
                    g = 4 * half + j
                    mm = pe.matmul(bank[32 * j:32 * j + 32], V1[:, s, g], PT[:, g], start=True, stop=True)
                mm.then_inc(filled[ring.bank(("PV", s, half))], 1)

            def values_to_tokens(s, half, it):
                transposes(("UT", s, half), [CU[:, half, r * P:(r + 1) * P] for r in range(REP)], it,
                           lambda it: [(cu_by_dve if half else cu_by_act, slot_n(s, it))])

            def attention_out(s, it):
                pe.wait_ge(cn_ready, 2 * slot_n(s, it))
                transposes(("CNT", s), [cn[:, c * P:(c + 1) * P] for c in range(KC)], it)
                bank = take(("WO", s), it, lambda it: [(ht_lo, ht_n(("CNT", s), it))])
                side = ht_side(("CNT", s))
                split_products(bank[:], lambda i, c: HT[:, i, c, side], lambda j, c: wo_s[:, j, c], KC).then_inc(
                    filled[ring.bank(("WO", s))], 1)

            def experts_down(s, it):
                pe.wait_ge(ht_lo, ht_n(("XT3", s), it))
                bank = take(("HG", s), it)
                split_products(bank[:, 0:HGW], lambda i, c: HT[:, i, c, s % 2], lambda j, c: ag_s[:, j, c],
                               KC).then_inc(filled[ring.bank(("HG", s))], 1)

            def base(s, it):
                split_products(take(("BASE", s), it)[:], lambda i, c: HT[:, i, c, s % 2], lambda j, c: wb_s[:, j, c],
                               KC, last=False)

            def experts_up(s, it):
                pe.wait_ge(hwt_lo, slot_n(s, it))
                split_products(psum[ring.bank(("BASE", s))][:], lambda i, c: HWT[:, s % 2, i], lambda j, c: mb_s[:, j],
                               1, first=False).then_inc(filled[ring.bank(("BASE", s))], 1)

            with pe.Fori(0, GROUPS, 1) as it:
                for s in range(SLOTS):
                    contexts(s, it)
                for s in range(SLOTS + 1):
                    if s < SLOTS:
                        normalized(0, s, it)
                    if s:
                        scores0(s - 1, it)
                for s in range(SLOTS):
                    context0(s, it)
                    keys_values(s, it)
                for p in range(SLOTS // 2):
                    normalized(1, 2 * p, it)
                    normalized(1, 2 * p + 1, it)
                    lora_down(p, it)
                    ffn0(2 * p, it)
                    ffn0(2 * p + 1, it)
                normalized(2, 0, it)
                queries(0, it)
                for s in range(SLOTS + 1):
                    if s < SLOTS:
                        keys_on_rows(s, it)
                        queries_on_rows(s, it)
                    if s:
                        max_on_rows(s - 1, it)
                    for g in range(G):
                        if s:
                            scores_less_max(s - 1, g, it)
                        if s < SLOTS:
                            scores_for_max(s, g, it)
                        if s and g == 5:
                            values(s - 1, 0, it)
                    if s + 1 < SLOTS:
                        normalized(2, s + 1, it)
                    if s:
                        values(s - 1, 1, it)
                    if s + 1 < SLOTS:
                        queries(s + 1, it)
                    if s:
                        values_to_tokens(s - 1, 0, it)
                        values_to_tokens(s - 1, 1, it)
                        attention_out(s - 1, it)
                normalized(3, 0, it)
                for s in range(SLOTS):
                    if s + 1 < SLOTS:
                        normalized(3, s + 1, it)
                    experts_down(s, it)
                    base(s, it)
                for s in range(SLOTS + 1):
                    if s < SLOTS:
                        pe.wait_ge(hw_ready, slot_n(s, it))
                        transposes(("HWT", s), [hgs[:, s, 0:ER]], it)
                    if s:
                        experts_up(s - 1, it)
                wait_each(lambda it: [drained(name, it) for name in ring.end_of_loop], it)


_INS = ["x", "ctx_4096", "itok_BxS2_0_2047", "g_xattn", "g_ffn", "L0_ffn_gate", "L0_ffn_kernel", "L0_ffn_bias",
        "L0_ffn_lora_A", "L0_ffn_lora_B", "L0_ffn_lora_A_shared", "L0_ffn_lora_B_shared", "L1_xattn_Wq",
        "L1_xattn_Wk", "L1_xattn_Wv", "L1_xattn_Wo", "L1_ffn_W_base", "L1_ffn_b_base", "L1_ffn_W_gate",
        "L1_ffn_W_thr", "L1_ffn_b_thr", "L1_ffn_A", "L1_ffn_B"]


def kernel(**inputs):
    import concourse.bacc as bacc
    from concourse.bass_utils import run_bass_kernel_spmd

    nc = bacc.Bacc("TRN2", target_bir_lowering=False, num_devices=1)
    arrays, args = {}, []
    for name in _INS:
        a = np.ascontiguousarray(inputs[name])
        arrays[f"in_{name}"] = a
        args.append(nc.dram_tensor(f"in_{name}", a.shape, mybir.dt.from_np(a.dtype), kind="ExternalInput").ap())
    args.append(nc.dram_tensor("out_0", (B, P, D), F32, kind="ExternalOutput").ap())
    build(nc, *args)
    r = run_bass_kernel_spmd(nc, [arrays], core_ids=[0])
    return r.results[0]["out_0"]
```

```python
from contextlib import ExitStack

import concourse.bass as bass
import numpy as np
from concourse import mybir

ALU = mybir.AluOpType
ACT = mybir.ActivationFunctionType
AX = mybir.AxisListType
F32 = mybir.dt.float32
F32R = mybir.dt.float32r
I32 = mybir.dt.int32

P = 128
B = 8
D = 512
KC = D // P
SLOTS = 4
GROUPS = B // SLOTS
NL, R0 = 16, 32
H, G, DH = 32, 8, 16
REP = H // G
E, R1 = 8, 16
ER = E * R1
HGW = ER + E + 2
EPS = 1e-5
ROPE_THETA = 10000.0
BANKS = 8


class PsumRing:

    def __init__(self, setup, loop):
        self.place, self.before, self.count = {}, {}, [0] * BANKS
        last = self.assign(setup, False, [None] * BANKS)
        before = list(self.count)
        self.end_of_loop = self.assign(loop, True, last)
        self.per = [a - b for a, b in zip(self.count, before)]

    def assign(self, uses, in_loop, last):
        last, held, b = list(last), {}, 0
        for name in uses:
            if name[0] == "FREE":
                del held[name[1]]
                continue
            while b in held.values():
                b = (b + 1) % BANKS
            self.place[name] = (b, self.count[b], in_loop)
            self.before[name] = last[b]
            self.count[b] += 1
            last[b] = name
            if name[0] == "BASE":
                held[name[1]] = b
            b = (b + 1) % BANKS
        return last

    def bank(self, name):
        return self.place[name][0]

    def nth(self, name, it):
        b, n, in_loop = self.place[name]
        return it * self.per[b] + n if in_loop else n


def setup_uses():
    u = [("GREP",)] + [("AEFF", c) for c in range(KC)] + [("LBT", c) for c in range(KC)]
    u += [("BEFF", h) for h in range(GROUPS)] + [("WBT", c) for c in range(KC)]
    u += [("AST",), ("BST",)] + [("AGT", c) for c in range(KC)] + [("MBT",)]
    return u


def loop_uses():
    u = [("CT", s) for s in range(SLOTS)]
    u += [("XT0", 0), ("XT0", 1), ("KV", 0), ("SIM", 0), ("XT0", 2), ("SIM", 1), ("XT0", 3), ("SIM", 2), ("SIM", 3),
          ("CTX0", 0), ("CTX0", 1), ("KV", 1), ("CTX0", 2), ("CTX0", 3), ("XT1", 0), ("XT1", 1), ("KV", 2),
          ("AX", 0), ("FFN0", 0), ("XT1", 2), ("FFN0", 1), ("XT1", 3), ("KV", 3), ("AX", 1), ("FFN0", 2), ("XT2", 0),
          ("FFN0", 3), ("XT2", 1), ("Q", 0), ("KT", 0), ("Q", 1), ("QN", 0), ("XT2", 2)]
    for s in range(SLOTS + 1):
        if s:
            u.append(("MT", s - 1))
        if s == 1:
            u.append(("XT2", 3))
        if s >= 3:
            u.append(("XT3", s - 3))
        if s >= 2:
            u += [("UT", s - 2, 0), ("UT", s - 2, 1)]
        if s < SLOTS:
            u += [("QT", s, gp) for gp in range(G // 2)]
        if 2 <= s < SLOTS:
            u.append(("CNT", s - 2))
        for g in range(G):
            if s:
                u.append(("S2", s - 1, g))
            if s < SLOTS:
                u.append(("S1", s, g))
            if s == SLOTS and g == 1:
                u.append(("CNT", s - 2))
            if s >= 2 and g == (5 if s == SLOTS else 2):
                u.append(("WO", s - 2))
            if s and g == 5:
                u.append(("PV", s - 1, 0))
        if s + 2 < SLOTS:
            u.append(("Q", s + 2))
        if s == 3:
            u += [("HG", 0), ("BASE", 0)]
        if s + 1 < SLOTS:
            u += [("KT", s + 1), ("QN", s + 1)]
        if s == SLOTS:
            u.append(("HG", 1))
        if s:
            u.append(("PV", s - 1, 1))
    u += [("XT3", 2), ("UT", 3, 0), ("UT", 3, 1), ("BASE", 1), ("HWT", 0), ("HWT", 1), ("CNT", 3), ("HG", 2),
          ("WO", 3), ("BASE", 2), ("XT3", 3), ("FREE", 0), ("FREE", 1), ("HG", 3), ("BASE", 3),
          ("HWT", 2), ("HWT", 3), ("FREE", 2), ("FREE", 3)]
    return u


HT_ORDER = ([("XT1", 0), ("XT1", 1), ("XT1", 2), ("XT1", 3), ("XT2", 0), ("XT2", 1), ("XT2", 2), ("XT2", 3)]
            + [("CNT", 0), ("XT3", 0), ("CNT", 1), ("XT3", 1), ("CNT", 2), ("XT3", 2), ("CNT", 3), ("XT3", 3)])
HT_SIDE = {("XT1", 0): 0, ("XT1", 1): 1, ("XT1", 2): 0, ("XT1", 3): 1, ("XT2", 0): 0, ("XT2", 1): 1, ("XT2", 2): 1,
           ("XT2", 3): 1, ("CNT", 0): 0, ("CNT", 1): 0, ("CNT", 2): 0, ("XT3", 0): 1, ("XT3", 1): 1, ("XT3", 2): 0,
           ("CNT", 3): 1, ("XT3", 3): 0}
XB3_ORDER = (1, 2, 0, 3)


GATE_STEPS = 10


def build(nc, x, ctx, pos, g_xattn, g_ffn, gate, w0, bias0, lora_a, lora_b, lora_as, lora_bs,
          wq, wk, wv, wo, w_base, b_base, w_gate, w_thr, b_thr, moe_a, moe_b, out):
    ring = PsumRing(setup_uses(), loop_uses())
    with ExitStack() as stack:
        def sb(name, shape, dt=F32):
            return stack.enter_context(nc.sbuf_tensor(name, [P] + shape, dt))

        def sem(name):
            return stack.enter_context(nc.semaphore(name))

        stack.enter_context(nc.allow_non_contiguous_dma(reason="small tables and LoRA factors"))

        ident = sb("ident", [P])
        mask_r = sb("mask_r", [R0])
        mask_g = sb("mask_g", [2])
        pick_g = sb("pick_g", [G], F32R)
        gate_t = sb("gate_t", [B])
        gate_rep = sb("gate_rep", [KC, B])
        tg = sb("tg", [4])
        bthr = sb("bthr", [1])
        half_neg = sb("half_neg", [1])
        eps_t = sb("eps_t", [1])
        wait_spot = sb("wait_spot", [1])
        gbias = sb("gbias", [2, D])
        pos_i = sb("pos_i", [B], I32)
        pos_f = sb("pos_f", [B])
        inv_f = sb("inv_f", [DH // 2])
        ang = sb("ang", [B, DH // 2])
        turns = sb("turns", [B, DH // 2])
        rope_cos = sb("rope_cos", [B, DH // 2])
        rope_sin = sb("rope_sin", [B, 2, DH // 2])

        w0_s = sb("w0_s", [2, KC, D], F32R)
        wq_s = sb("wq_s", [2, KC, D], F32R)
        wo_s = sb("wo_s", [2, KC, D], F32R)
        wb_s = sb("wb_s", [2, KC, D], F32R)
        mb_s = sb("mb_s", [2, D], F32R)
        ag_s = sb("ag_s", [2, KC, HGW], F32R)
        wkv = sb("wkv", [KC, 2 * G * DH])
        a_eff = sb("a_eff", [KC, B, R0])
        b_eff = sb("b_eff", [GROUPS, D])
        a_cat = sb("a_cat", [2, KC, 4, R0], F32R)
        b_cat = sb("b_cat", [2, D], F32R)
        b_raw = sb("b_raw", [D])

        X = sb("X", [SLOTS, D])
        XB = sb("XB", [SLOTS, D])
        C = sb("C", [SLOTS, D])
        V1 = sb("V1", [SLOTS, G, 32])
        KO = sb("KO", [SLOTS, G * DH])
        XN = sb("XN", [2, D])
        HT = sb("HT", [2, KC, 2, P], F32R)
        KT1 = sb("KT1", [2, 2, G * DH])
        KS = sb("KS", [G // 2, 2, 2, 32])
        QN = sb("QN", [2, REP * P], F32R)
        sel_q = sb("sel_q", [G // 2, 6, 32], F32R)
        PR = sb("PR", [SLOTS, P])
        QT = sb("QT", [2, G // 2, REP * P], F32R)
        KBD = sb("KBD", [2, G // 2, 2, P], F32R)
        NM = sb("NM", [REP, G])
        NMHL = sb("NMHL", [REP, 2 * G])
        MT = sb("MT", [REP * P], F32R)
        PT = sb("PT", [G, REP * P])
        CU = sb("CU", [2, REP * P])
        RS = sb("RS", [2, REP, REP])
        AXT = sb("AXT", [2, 2, P], F32R)
        HWT = sb("HWT", [2, 2, P], F32R)
        stats = sb("stats", [2, 6])
        mv = sb("mv", [2, 2])
        ve = sb("ve", [2, 1])
        rstd = sb("rstd", [2, 1])
        smx = sb("smx", [SLOTS, 4])
        gt = sb("gt", [SLOTS, E + 1])
        gd = sb("gd", [SLOTS, 12])
        gw = sb("gw", [2, SLOTS, E])

        ct = PT[:, 0:SLOTS].rearrange("p s (c t) -> p s c t", c=KC)
        xt0 = CU[:].rearrange("p s (c t) -> p s c t", c=KC)
        qr = XB[:, 2:4]
        QO = XB[:, 1]
        cn = XB[:, 0]
        hgs = [KT1[:].rearrange("p a b n -> p (a b n)")[:, 0:2 * HGW].rearrange("p (s n) -> p s n", s=2),
               KO[:].rearrange("p a n -> p (a n)")[:, 0:2 * HGW].rearrange("p (s n) -> p s n", s=2)]
        lora_a_nat, lora_b_t = PT[:, 0:4], PT[:, 4:8]
        lora_b_nat = XB
        w_base_nat = PT[:, 0:4]
        wq_raw, wo_raw = X[:], C[:]
        moe_a_nat, gate_nat, as_nat, moe_b_nat = XB[:, 0], XB[:, 1], XB[:, 2], XB[:, 3]
        bs_nat = PR[:].rearrange("p a (b r) -> p (a b) r", r=R0)[:, 0:KC]
        spread_n = KO
        gsel = V1[:].rearrange("p s g j -> p (s g j)").rearrange("p (k b r) -> p k b r", k=KC, b=B)

        psum = [stack.enter_context(nc.psum_tensor(f"bank{n}", [P, 512], F32)) for n in range(BANKS)]

        filled = [sem(f"filled{n}") for n in range(BANKS)]
        pos_in, gate_in, bias_in, lora_a_in, lora_b_in, w_kv_in, w0_in, wq_in, w_base_in, wo_in, small_in, bs_in = (
            sem(n) for n in ("pos_in", "gate_in", "bias_in", "lora_a_in", "lora_b_in", "w_kv_in", "w0_in", "wq_in",
                             "w_base_in", "wo_in", "small_in", "bs_in"))
        x_in = [sem(f"x_in{s}") for s in range(SLOTS)]
        ctx_in = [sem(f"ctx_in{s}") for s in range(SLOTS)]
        out_stored = [sem(f"out_stored{s}") for s in range(SLOTS)]
        names = ("ident_made", "spread_made", "tables_made", "masks_made", "rope_args", "trig_done", "sin_signed",
                 "gates_done", "gbias_made", "gate_rep_done", "lbt_done", "gsel_made", "aeff_done", "beff_done",
                 "w0_hi", "w0_lo", "wq_hi", "wq_lo", "wo_hi", "wo_lo", "wb_hi", "wb_lo", "ast_hi", "ast_lo",
                 "braw_shared", "agt_hi", "agt_lo", "mbt_hi", "mbt_lo", "v1_ready", "mt_zeroed", "rope_step",
                 "gates_in", "pool_step", "one_plus")
        (ident_made, spread_made, tables_made, masks_made, rope_args, trig_done, sin_signed, gates_done,
         gbias_made, gate_rep_done, lbt_done, gsel_made, aeff_done, beff_done, w0_hi, w0_lo, wq_hi, wq_lo, wo_hi,
         wo_lo, wb_hi, wb_lo, ast_hi, ast_lo, braw_shared, agt_hi, agt_lo, mbt_hi, mbt_lo, v1_ready, mt_zeroed,
         rope_step, gates_in, pool_step, one_plus) = (sem(n) for n in names)
        ln_stats, ln_var, ln_eps, ln_rstd, xn_ready, resid_done = (
            sem(n) for n in ("ln_stats", "ln_var", "ln_eps", "ln_rstd", "xn_ready", "resid_done"))
        ct_ready, xt0_ready, max0_ready, exp0_done, sum0_inv, p0_ready = (
            sem(n) for n in ("ct_ready", "xt0_ready", "max0_ready", "exp0_done", "sum0_inv", "p0_ready"))
        ht_hi, ht_lo, acat_hi, acat_lo, braw_ready, bcat_hi, bcat_lo, axt_hi, axt_lo, xb_ready = (
            sem(n) for n in ("ht_hi", "ht_lo", "acat_hi", "acat_lo", "braw_ready", "bcat_hi", "bcat_lo", "axt_hi",
                             "axt_lo", "xb_ready"))
        (k_prod, ko_ready, v_ready, ks_hi, ks_lo, kbd_ready, q_prod, qo_ready, qn_hi, qn_lo, qt_done,
         max1_done, nm_hi, nm_lo, mt_ready, exp1_done, cu_by_act, cu_by_dve, rs_ready, cn_ready) = (
             sem(n) for n in (
                 "k_prod", "ko_ready", "v_ready", "ks_hi", "ks_lo", "kbd_ready", "q_prod", "qo_ready", "qn_hi",
                 "qn_lo", "qt_done", "max1_done", "nm_hi", "nm_lo", "mt_ready", "exp1_done",
                 "cu_by_act", "cu_by_dve", "rs_ready", "cn_ready"))
        hg_ready, base_done, gate_args, gate_exp, gate_step, hw_ready, hwt_hi, hwt_lo, xb3_ready = (
            sem(n) for n in ("hg_ready", "base_done", "gate_args", "gate_exp", "gate_step", "hw_ready", "hwt_hi",
                             "hwt_lo", "xb3_ready"))

        def filled_at(name, it=0):
            return filled[ring.bank(name)], ring.nth(name, it) + 1

        def drained(name, it=0):
            step, s = name[0], (name[1] if len(name) > 1 else 0)
            return {
                "GREP": lambda: (gate_rep_done, 1),
                "LBT": lambda: (lbt_done, s + 1),
                "AEFF": lambda: (aeff_done, s + 1),
                "BEFF": lambda: (beff_done, s + 1),
                "AST": lambda: (ast_lo, 1),
                "BST": lambda: (braw_shared, 2),
                "AGT": lambda: (agt_lo, s + 1),
                "MBT": lambda: (mbt_lo, 1),
                "WBT": lambda: (wb_lo, s + 1),
                "CT": lambda: (ct_ready, slot_n(s, it)),
                "XT0": lambda: (xt0_ready, slot_n(s, it)),
                "SIM": lambda: (exp0_done, slot_n(s, it)),
                "CTX0": lambda: (resid_done, ln_n(0, s, it)),
                "KV": lambda: (v_ready, slot_n(s, it)),
                "XT1": lambda: (ht_lo, ht_n(name, it)),
                "AX": lambda: (axt_lo, pair_n(s, it)),
                "FFN0": lambda: (resid_done, ln_n(1, s, it)),
                "XT2": lambda: (ht_lo, ht_n(name, it)),
                "Q": lambda: (q_prod, 2 * slot_n(s, it)),
                "KT": lambda: (kbd_ready, 2 * slot_n(s, it)),
                "QN": lambda: (qn_lo, slot_n(s, it)),
                "QT": lambda: (qt_done, it * (G // 2) * SLOTS + (G // 2 * s + name[2] + 1)),
                "MT": lambda: (mt_ready, slot_n(s, it)),
                "S1": lambda: (max1_done, it * G * SLOTS + (G * s + name[2] + 1)),
                "S2": lambda: (exp1_done, it * G * SLOTS + (G * s + name[2] + 1)),
                "PV": lambda: (cu_by_dve if name[2] else cu_by_act, slot_n(s, it)),
                "UT": lambda: (cn_ready, it * 2 * SLOTS + (2 * s + name[2] + 1)),
                "CNT": lambda: (ht_lo, ht_n(name, it)),
                "WO": lambda: (resid_done, ln_n(2, s, it)),
                "XT3": lambda: (ht_lo, ht_n(name, it)),
                "HG": lambda: (hg_ready, slot_n(s, it)),
                "BASE": lambda: (resid_done, ln_n(3, s, it)),
                "HWT": lambda: (hwt_lo, slot_n(s, it)),
            }[step]()

        def pair_n(p, it):
            return it * (SLOTS // 2) + (p + 1)

        def ln_n(layer, s, it):
            return it * 4 * SLOTS + (layer * SLOTS + s + 1)

        def ht_n(name, it):
            return it * len(HT_ORDER) + (HT_ORDER.index(name) + 1)

        def xb3_n(s, it):
            return it * SLOTS + (XB3_ORDER.index(s) + 1)

        def slot_n(s, it):
            return it * SLOTS + (s + 1)

        block = stack.enter_context(nc.Block())


        @block.sync
        def _(sp):
            lora_b_v = lora_b.rearrange("n (c p) r -> p c n r", p=P)
            lora_b_nat_v = lora_b_nat[:].rearrange("p c (n r) -> p c n r", n=NL)
            w0_v = w0.rearrange("(c p) n -> p c n", p=P)
            for c in range(KC):
                sp.dma_start(lora_b_nat_v[:, c], lora_b_v[:, c]).then_inc(lora_b_in, 16)
            sp.dma_start(CU[:], w0_v[:, 0:2]).then_inc(w0_in, 16)
            sp.dma_start(XN[:], w0_v[:, 2:4]).then_inc(w0_in, 16)
            sp.dma_start(wo_raw, wo.rearrange("(c p) n -> p c n", p=P)).then_inc(wo_in, 16)
            sp.dma_start(wkv[:, :, 0:P], wk.rearrange("(c p) n -> p c n", p=P)).then_inc(w_kv_in, 16)
            sp.dma_start(wkv[:, :, P:2 * P], wv.rearrange("(c p) n -> p c n", p=P)).then_inc(w_kv_in, 16)
            sp.wait_ge(*filled_at(("AEFF", KC - 1)))
            sp.dma_start(w_base_nat, w_base.rearrange("(c p) n -> p c n", p=P)).then_inc(w_base_in, 16)
            sp.wait_ge(*filled_at(("LBT", KC - 1)))
            sp.dma_start(moe_a_nat, moe_a.rearrange("e r d -> (e r) d")).then_inc(small_in, 16)
            sp.dma_start(gate_nat[0:E], w_gate).then_inc(small_in, 16)
            sp.dma_start(gate_nat[E:E + 1], w_thr).then_inc(small_in, 16)
            sp.dma_start(gate_nat[E + 1:E + 2], w_thr).then_inc(small_in, 16)
            sp.dma_start(as_nat[0:R0], lora_as).then_inc(small_in, 16)
            moe_b_v = moe_b.rearrange("e (c p) r -> p c e r", p=P)
            moe_b_nat_v = moe_b_nat.rearrange("p (c e r) -> p c e r", c=KC, e=E)
            for c in range(KC):
                sp.dma_start(moe_b_nat_v[:, c], moe_b_v[:, c]).then_inc(small_in, 16)
            sp.wait_ge(wq_hi, 1)
            sp.wait_ge(wq_lo, 1)
            for s in range(SLOTS):
                sp.dma_start(X[:, s], x[s]).then_inc(x_in[s], 16)
            sp.wait_ge(wo_hi, 1)
            sp.wait_ge(wo_lo, 1)
            for s in range(SLOTS):
                sp.dma_start(C[:, s], ctx[s]).then_inc(ctx_in[s], 16)

            def store_group(it):
                for s in range(SLOTS):
                    sp.wait_ge(resid_done, ln_n(3, s, it))
                    sp.dma_start(out[it * SLOTS + s], XB[:, s]).then_inc(out_stored[s], 16)

            with sp.Fori(0, GROUPS - 1, 1) as it:
                for s in range(SLOTS):
                    sp.wait_ge(*filled_at(("CTX0", s), it))
                    sp.dma_start(C[:, s], ctx[(it + 1) * SLOTS + s]).then_inc(ctx_in[s], 16)
                for s in XB3_ORDER:
                    sp.wait_ge(xb3_ready, xb3_n(s, it))
                    sp.wait_ge(xn_ready, ln_n(3, s, it))
                    sp.dma_start(X[:, s], x[(it + 1) * SLOTS + s]).then_inc(x_in[s], 16)
                store_group(it)
            store_group(GROUPS - 1)
            for s in range(SLOTS):
                sp.wait_ge(out_stored[s], 16 * (GROUPS + 1))

        @block.gpsimd
        def _(pool):
            for s in range(SLOTS):
                pool.sem_inc(out_stored[s], 16)
            pool.memset(ident[:], 0.0).then_inc(pool_step, 1)
            pool.memset(spread_n[0:NL], 1.0).then_inc(pool_step, 1)
            pool.wait_ge(pool_step, 1)
            pool.affine_select(out=ident[:], in_=ident[:], compare_op=ALU.not_equal, fill=1.0, base=0,
                               pattern=[[-1, P]], channel_multiplier=1).then_inc(ident_made, 1)
            pool.wait_ge(pool_step, 2)
            pool.affine_select(out=spread_n[0:NL], in_=spread_n[0:NL], compare_op=ALU.is_ge, fill=0.0, base=0,
                               pattern=[[P, KC], [1, P]], channel_multiplier=-R0).then_inc(pool_step, 1)
            pool.wait_ge(pool_step, 3)
            pool.affine_select(out=spread_n[0:NL], in_=spread_n[0:NL], compare_op=ALU.is_ge, fill=0.0, base=R0 - 1,
                               pattern=[[-P, KC], [-1, P]], channel_multiplier=R0).then_inc(spread_made, 1)
            pool.memset(half_neg[:], -0.5).then_inc(tables_made, 1)
            pool.memset(eps_t[:], EPS).then_inc(tables_made, 1)
            for j in range(DH // 2):
                inv = np.float32(1.0) / np.float32(ROPE_THETA) ** np.float32(2 * j / DH)
                pool.memset(inv_f[:, j:j + 1], float(inv)).then_inc(tables_made, 1)
            pool.memset(MT[:].bitcast(F32), 0.0).then_inc(mt_zeroed, 1)
            pool.wait_ge(masks_made, 1)
            pool.wait_ge(gate_rep_done, 1)
            pool.tensor_tensor(gsel, mask_r[:].unsqueeze(1).unsqueeze(1).to_broadcast([P, KC, B, R0]),
                               gate_rep[:].unsqueeze(3).to_broadcast([P, KC, B, R0]), ALU.mult).then_inc(gsel_made, 1)
            pool.wait_ge(gates_done, 1)
            pool.wait_ge(bias_in, 32)
            for layer in range(2):
                pool.tensor_scalar(gbias[:, layer], gbias[:, layer], tg[:, 2 + layer:3 + layer], 0.0, ALU.mult,
                                   ALU.add).then_inc(gbias_made, 1)
            pool.wait_ge(*filled_at(("BEFF", GROUPS - 1)))
            pool.memset(V1[:], 0.0).then_inc(pool_step, 1)
            pool.wait_ge(pool_step, 4)
            pool.memset(V1[:, :, :, DH:DH + 1], 1.0).then_inc(v1_ready, 1)

            def ln_scale(layer, s, it):
                pool.wait_ge(ln_var, ln_n(layer, s, it))
                pool.tensor_tensor(ve[:, s % 2], mv[:, s % 2, 1:2], eps_t[:], ALU.add).then_inc(ln_eps, 1)
                pool.wait_ge(ln_eps, ln_n(layer, s, it))
                pool.tensor_tensor(rstd[:, s % 2], ve[:, s % 2], half_neg[:], ALU.pow).then_inc(ln_rstd, 1)

            def add_bias(layer, s, it):
                if layer == 0:
                    pool.wait_ge(resid_done, ln_n(0, s, it))
                    pool.wait_ge(out_stored[s], 16 * (it + 1))
                else:
                    pool.wait_ge(resid_done, ln_n(2, s, it))
                pool.tensor_tensor(XB[:, s], X[:, s], gbias[:, layer], ALU.add).then_inc(
                    xb3_ready if layer else xb_ready, 1)

            def rotate(dst, a, b, done):
                pool.tensor_tensor(dst[0], a[0], b[1], ALU.add).then_inc(done, 1)
                pool.tensor_tensor(dst[1], a[1], b[0], ALU.add).then_inc(done, 1)

            def k_add(s, it):
                pool.wait_ge(k_prod, 2 * slot_n(s, it))
                a, b = (KT1[:, s % 2, j].rearrange("p (g h d) -> p h g d", g=G, h=2) for j in range(2))
                o = KO[:, s].rearrange("p (g h d) -> p h g d", g=G, h=2)
                rotate([o[:, 0], o[:, 1]], [a[:, 0], a[:, 1]], [b[:, 0], b[:, 1]], ko_ready)

            def k_lo(s, it):
                pool.wait_ge(ks_hi, slot_n(s, it))
                pool.tensor_tensor(KS[:, :, :, 1], KO[:, s].rearrange("p (g n) -> p g n", n=32).unsqueeze(2)
                                   .to_broadcast([P, G // 2, 2, 32]), KS[:, :, :, 0], ALU.subtract).then_inc(ks_lo, 1)

            def q_add(s, it):
                pool.wait_ge(q_prod, 2 * slot_n(s, it))
                if s:
                    pool.wait_ge(*filled_at(("QN", s - 1), it))
                a, b = (qr[:, j].rearrange("p (g r h d) -> p h g r d", g=G, r=REP, h=2) for j in range(2))
                o = QO.rearrange("p (r g h d) -> p h g r d", g=G, r=REP, h=2)
                rotate([o[:, 0], o[:, 1]], [a[:, 0], a[:, 1]], [b[:, 0], b[:, 1]], qo_ready)

            with pool.Fori(0, GROUPS, 1) as it:
                for s in range(SLOTS):
                    ln_scale(0, s, it)
                ln_scale(1, 0, it)
                ln_scale(1, 1, it)
                k_add(0, it)
                pool.wait_ge(gbias_made, 2)
                add_bias(0, 0, it)
                ln_scale(1, 2, it)
                ln_scale(1, 3, it)
                add_bias(0, 1, it)
                k_add(1, it)
                k_add(2, it)
                add_bias(0, 2, it)
                ln_scale(2, 0, it)
                add_bias(0, 3, it)
                ln_scale(2, 1, it)
                k_add(3, it)
                ln_scale(2, 2, it)
                ln_scale(2, 3, it)
                k_lo(0, it)
                q_add(0, it)
                for s in range(SLOTS + 1):
                    if s + 1 < SLOTS:
                        q_add(s + 1, it)
                        k_lo(s + 1, it)
                    if s >= 2:
                        ln_scale(3, s - 2, it)
                pool.wait_ge(*filled_at(("QN", SLOTS - 1), it))
                add_bias(1, 1, it)
                add_bias(1, 2, it)
                pool.wait_ge(*filled_at(("CNT", SLOTS - 1), it))
                add_bias(1, 0, it)
                ln_scale(3, 3, it)
                add_bias(1, 3, it)

        @block.scalar
        def _(act):
            act.dma_start(gate_t[0:NL], gate.rearrange("b n -> n b")).then_inc(gate_in, 16)
            act.dma_start(lora_a_nat, lora_a.rearrange("n r d -> (n r) d").rearrange("(c p) d -> p c d", p=P)).then_inc(
                lora_a_in, 16)
            act.dma_start(pos_i[:], pos.rearrange("b t -> t b")).then_inc(pos_in, 16)
            act.dma_start(wq_raw, wq.rearrange("(c p) n -> p c n", p=P)).then_inc(wq_in, 16)
            act.dma_start(tg[:, 0:2], g_xattn.unsqueeze(0).to_broadcast([P, 2])).then_inc(gates_in, 16)
            act.dma_start(tg[:, 2:4], g_ffn.unsqueeze(0).to_broadcast([P, 2])).then_inc(gates_in, 16)
            act.dma_start(bthr[:], b_thr.unsqueeze(0).to_broadcast([P, 1])).then_inc(gates_in, 16)
            act.dma_start(gbias[:, 0], bias0.unsqueeze(0).to_broadcast([P, D])).then_inc(bias_in, 16)
            act.dma_start(gbias[:, 1], b_base.unsqueeze(0).to_broadcast([P, D])).then_inc(bias_in, 16)
            act.dma_start(bs_nat, lora_bs.rearrange("(c p) r -> p c r", p=P)).then_inc(bs_in, 16)

            def copy(out_ap, in_ap):
                return act.activation(out_ap, in_ap, ACT.Copy)

            act.wait_ge(rope_args, 2)
            act.activation(rope_sin[:, :, 0], ang[:], ACT.Sin).then_inc(trig_done, 1)
            act.activation(rope_cos[:], turns[:], ACT.Sin).then_inc(trig_done, 1)
            for c in range(KC):
                act.wait_ge(*filled_at(("AEFF", c)))
                copy(a_eff[:, c], psum[ring.bank(("AEFF", c))][:, 0:B * R0].rearrange("p (b r) -> p b r", b=B)
                     ).then_inc(aeff_done, 1)
            act.wait_ge(w0_in, 32)
            copy(w0_s[:, 0, 0:2], CU[:]).then_inc(w0_hi, 1)
            copy(w0_s[:, 0, 2:4], XN[:]).then_inc(w0_hi, 1)
            act.wait_ge(gates_in, 48)
            act.activation(tg[:], tg[:], ACT.Tanh).then_inc(gates_done, 1)
            act.wait_ge(wq_in, 16)
            copy(wq_s[:, 0], wq_raw).then_inc(wq_hi, 1)
            act.wait_ge(wo_in, 16)
            copy(wo_s[:, 0], wo_raw).then_inc(wo_hi, 1)
            for c in range(KC):
                act.wait_ge(*filled_at(("WBT", c)))
                copy(wb_s[:, 0, c], psum[ring.bank(("WBT", c))][:]).then_inc(wb_hi, 1)
            act.wait_ge(*filled_at(("AST",)))
            shared_a = psum[ring.bank(("AST",))][:, 0:KC * R0].rearrange("p (c r) -> p c r", c=KC).unsqueeze(2)
            copy(a_cat[:, 0, :, 1::2], shared_a.to_broadcast([P, KC, 2, R0])).then_inc(ast_hi, 1)
            for c in range(KC):
                act.wait_ge(*filled_at(("AGT", c)))
                copy(ag_s[:, 0, c], psum[ring.bank(("AGT", c))][:, 0:HGW]).then_inc(agt_hi, 1)
            act.wait_ge(*filled_at(("MBT",)))
            copy(mb_s[:, 0], psum[ring.bank(("MBT",))][:]).then_inc(mbt_hi, 1)

            def hi_of_transposed(name, it):
                act.wait_ge(*filled_at(name, it))
                copy(HT[:, 0, :, HT_SIDE[name]], psum[ring.bank(name)][:].rearrange("p (c t) -> p c t", c=KC)
                     ).then_inc(ht_hi, 1)

            def exp0(s, it):
                act.wait_ge(max0_ready, slot_n(s, it))
                act.activation(PR[:, s], psum[ring.bank(("SIM", s))][:, 0:P], ACT.Exp, bias=smx[:, s, 0:1],
                               accum_out=smx[:, s, 1:2]).then_inc(exp0_done, 1)

            def xt0_copy(s, it):
                act.wait_ge(*filled_at(("XT0", s), it))
                act.activation(xt0[:, s % 2], psum[ring.bank(("XT0", s))][:].rearrange("p (c t) -> p c t", c=KC),
                               ACT.Copy, scale=P ** -0.5).then_inc(xt0_ready, 1)

            def a_cat_hi(p, it):
                if p:
                    act.wait_ge(*filled_at(("AX", p - 1), it))
                copy(a_cat[:, 0, :, 0::2], a_eff[:, :, bass.ds(it * SLOTS + 2 * p, 2)]).then_inc(acat_hi, 1)

            def b_cat_hi(p, it):
                act.wait_ge(braw_ready, 2 * pair_n(p, it))
                copy(b_cat[:, 0], b_raw[:]).then_inc(bcat_hi, 1)

            def keys_hi(s, it):
                act.wait_ge(ko_ready, 2 * slot_n(s, it))
                if s:
                    act.wait_ge(*filled_at(("KT", s - 1), it))
                copy(KS[:, :, :, 0].bitcast(F32R), KO[:, s].rearrange("p (g n) -> p g n", n=32).unsqueeze(2)
                     .to_broadcast([P, G // 2, 2, 32])).then_inc(ks_hi, 1)

            def value_heads(s, it):
                act.wait_ge(k_prod, 2 * slot_n(s, it))
                copy(V1[:, s, :, 0:DH], psum[ring.bank(("KV", s))][:, P:2 * P].rearrange("p (g d) -> p g d", g=G)
                     ).then_inc(v_ready, 1)

            def axt_hi_part(p, it):
                act.wait_ge(*filled_at(("AX", p), it))
                copy(AXT[:, 0], psum[ring.bank(("AX", p))][:, 0:2 * P].rearrange("p (s t) -> p s t", s=2)
                     ).then_inc(axt_hi, 1)

            def key_blocks(s, it):
                act.wait_ge(*filled_at(("KT", s), it))
                for g2 in range(2):
                    act.activation(KBD[:, s % 2, :, g2], psum[ring.bank(("KT", s))][:].rearrange(
                        "p (g t) -> p g t", g=G // 2), ACT.Copy, scale=mask_g[:, g2:g2 + 1]).then_inc(kbd_ready, 1)

            def queries_hi(s, it):
                act.wait_ge(*filled_at(("QN", s), it))
                copy(QN[:, 0], psum[ring.bank(("QN", s))][:]).then_inc(qn_hi, 1)

            def experts_to_sbuf(s, it):
                act.wait_ge(*filled_at(("HG", s), it))
                copy(hgs[s // 2][:, s % 2], psum[ring.bank(("HG", s))][:, 0:HGW]).then_inc(hg_ready, 1)

            def gate_exponentials(p, it):
                act.wait_ge(gate_args, 2 * pair_n(p, it))
                act.activation(gt[:, 2 * p:2 * p + 2], gt[:, 2 * p:2 * p + 2], ACT.Exp).then_inc(gate_exp, 1)

            def hi_of_experts(s, it):
                act.wait_ge(*filled_at(("HWT", s), it))
                copy(HWT[:, s % 2, 0], psum[ring.bank(("HWT", s))][:, 0:P]).then_inc(hwt_hi, 1)

            with act.Fori(0, GROUPS, 1) as it:
                a_cat_hi(0, it)
                for s in range(SLOTS):
                    act.wait_ge(*filled_at(("CT", s), it))
                    copy(ct[:, s], psum[ring.bank(("CT", s))][:].rearrange("p (c t) -> p c t", c=KC)).then_inc(
                        ct_ready, 1)
                xt0_copy(0, it)
                xt0_copy(1, it)
                exp0(0, it)
                xt0_copy(2, it)
                exp0(1, it)
                xt0_copy(3, it)
                value_heads(0, it)
                exp0(2, it)
                exp0(3, it)
                b_cat_hi(0, it)
                keys_hi(0, it)
                hi_of_transposed(("XT1", 0), it)
                hi_of_transposed(("XT1", 1), it)
                value_heads(1, it)
                axt_hi_part(0, it)
                value_heads(2, it)
                a_cat_hi(1, it)
                hi_of_transposed(("XT1", 2), it)
                hi_of_transposed(("XT1", 3), it)
                b_cat_hi(1, it)
                axt_hi_part(1, it)
                value_heads(3, it)
                hi_of_transposed(("XT2", 0), it)
                hi_of_transposed(("XT2", 1), it)
                key_blocks(0, it)
                queries_hi(0, it)
                hi_of_transposed(("XT2", 2), it)
                for s in range(SLOTS + 1):
                    if s:
                        act.wait_ge(*filled_at(("MT", s - 1), it))
                        copy(MT[0:2 * G], psum[ring.bank(("MT", s - 1))][0:2 * G]).then_inc(mt_ready, 1)
                    if s == 1:
                        hi_of_transposed(("XT2", 3), it)
                    if s >= 3:
                        hi_of_transposed(("XT3", s - 3), it)
                    if s < SLOTS:
                        for gp in range(G // 2):
                            act.wait_ge(*filled_at(("QT", s, gp), it))
                            copy(QT[:, s % 2, gp], psum[ring.bank(("QT", s, gp))][:]).then_inc(qt_done, 1)
                    if 2 <= s < SLOTS:
                        hi_of_transposed(("CNT", s - 2), it)
                    if s:
                        for g in range(G):
                            act.wait_ge(*filled_at(("S2", s - 1, g), it))
                            act.activation(PT[:, g], psum[ring.bank(("S2", s - 1, g))][:], ACT.Exp).then_inc(
                                exp1_done, 1)
                            if g == 1 and s == SLOTS:
                                hi_of_transposed(("CNT", s - 2), it)
                            if g == 3 and s + 1 < SLOTS:
                                keys_hi(s + 1, it)
                    if s == 0:
                        keys_hi(1, it)
                    if s:
                        act.wait_ge(*filled_at(("PV", s - 1, 0), it))
                        copy(CU[:, 0], psum[ring.bank(("PV", s - 1, 0))][:]).then_inc(cu_by_act, 1)
                    if s == 3:
                        experts_to_sbuf(0, it)
                    if s + 1 < SLOTS:
                        queries_hi(s + 1, it)
                        key_blocks(s + 1, it)
                experts_to_sbuf(1, it)
                hi_of_transposed(("XT3", 2), it)
                gate_exponentials(0, it)
                hi_of_experts(0, it)
                hi_of_experts(1, it)
                hi_of_transposed(("CNT", 3), it)
                experts_to_sbuf(2, it)
                hi_of_transposed(("XT3", 3), it)
                experts_to_sbuf(3, it)
                gate_exponentials(1, it)
                hi_of_experts(2, it)
                hi_of_experts(3, it)

        @block.vector
        def _(dve):
            def recip(out_ap, in_ap):
                return dve.reciprocal(out_ap, in_ap)

            round_up = 1.5 * 2.0 ** 23
            c1, c2 = 6.28125, float(np.float32(2 * np.pi - 6.28125))
            c3 = float(np.float32(2 * np.pi - 6.28125 - c2))
            below_pi = 3.1415925
            step = [0]

            def rope(ins):
                step[0] += 1
                ins.then_inc(rope_step, 1)
                dve.wait_ge(rope_step, step[0])

            dve.wait_ge(ident_made, 1)
            dve.tensor_reduce(mask_r[:], ident[:].rearrange("p (j r) -> p r j", r=R0), AX.X, ALU.add).then_inc(
                masks_made, 1)
            dve.tensor_reduce(mask_g[:], ident[:].rearrange("p (q g d) -> p g q d", g=2, d=DH), AX.XY, ALU.add
                              ).then_inc(masks_made, 1)
            dve.wait_ge(*filled_at(("GREP",)))
            dve.tensor_copy(gate_rep[:].rearrange("p k b -> p (k b)"), psum[ring.bank(("GREP",))][:, 0:KC * B]
                            ).then_inc(gate_rep_done, 1)
            dve.tensor_tensor(pick_g[:], ident[:, 0:G], ident[:, G:2 * G], ALU.add).then_inc(masks_made, 1)
            blocks = ident[:].rearrange("p (g n) -> p g n", n=32).unsqueeze(2).to_broadcast([P, G // 2, 2, 32])
            for first, scale in ((0, DH ** -0.5), (2, 0.0), (4, DH ** -0.5)):
                dve.tensor_scalar(sel_q[:, :, first:first + 2], blocks, scale, None, ALU.mult).then_inc(masks_made, 1)
            dve.wait_ge(tables_made, 2 + DH // 2)
            dve.wait_ge(pos_in, 16)
            rope(dve.tensor_copy(pos_f[:], pos_i[:]))
            rope(dve.tensor_tensor(ang[:], pos_f[:].unsqueeze(2).to_broadcast([P, B, DH // 2]),
                                   inv_f[:].unsqueeze(1).to_broadcast([P, B, DH // 2]), ALU.mult))
            rope(dve.tensor_scalar(turns[:], ang[:], float(1 / (2 * np.pi)), round_up, ALU.mult, ALU.add))
            rope(dve.tensor_scalar(turns[:], turns[:], -round_up, None, ALU.add))
            for c in (c1, c2, c3):
                rope(dve.scalar_tensor_tensor(out=ang[:], in0=turns[:], scalar=-c, in1=ang[:], op0=ALU.mult,
                                              op1=ALU.add))
            rope(dve.tensor_scalar(ang[:], ang[:], below_pi, -below_pi, ALU.min, ALU.max))
            dve.scalar_tensor_tensor(out=turns[:], in0=ang[:], scalar=-1.0, in1=ang[:], op0=ALU.mult, op1=ALU.max
                                     ).then_inc(rope_args, 1)
            dve.wait_ge(rope_args, 1)
            dve.tensor_scalar(turns[:], turns[:], -1.0, float(np.pi / 2), ALU.mult, ALU.add).then_inc(rope_args, 1)
            dve.wait_ge(trig_done, 1)
            dve.tensor_scalar(rope_sin[:, :, 1], rope_sin[:, :, 0], -1.0, None, ALU.mult).then_inc(sin_signed, 1)

            def minus_hi(lo_ap, whole, hi_ap):
                return dve.tensor_tensor(lo_ap, whole, hi_ap.bitcast(F32), ALU.subtract)

            for c in range(KC):
                dve.wait_ge(*filled_at(("LBT", c)))
                dve.tensor_copy(lora_b_t[:, c], psum[ring.bank(("LBT", c))][:]).then_inc(lbt_done, 1)
            dve.wait_ge(w0_hi, 2)
            minus_hi(w0_s[:, 1, 0:2], CU[:], w0_s[:, 0, 0:2]).then_inc(w0_lo, 1)
            minus_hi(w0_s[:, 1, 2:4], XN[:], w0_s[:, 0, 2:4]).then_inc(w0_lo, 1)
            dve.wait_ge(wq_hi, 1)
            minus_hi(wq_s[:, 1], wq_raw, wq_s[:, 0]).then_inc(wq_lo, 1)
            dve.wait_ge(wo_hi, 1)
            minus_hi(wo_s[:, 1], wo_raw, wo_s[:, 0]).then_inc(wo_lo, 1)
            for h in range(GROUPS):
                dve.wait_ge(*filled_at(("BEFF", h)))
                dve.tensor_copy(b_eff[:, h], psum[ring.bank(("BEFF", h))][:]).then_inc(beff_done, 1)
            for c in range(KC):
                dve.wait_ge(wb_hi, c + 1)
                minus_hi(wb_s[:, 1, c], psum[ring.bank(("WBT", c))][:], wb_s[:, 0, c]).then_inc(wb_lo, 1)
            dve.wait_ge(ast_hi, 1)
            shared_a = psum[ring.bank(("AST",))][:, 0:KC * R0].rearrange("p (c r) -> p c r", c=KC).unsqueeze(2)
            minus_hi(a_cat[:, 1, :, 1::2], shared_a.to_broadcast([P, KC, 2, R0]), a_cat[:, 0, :, 1::2]).then_inc(
                ast_lo, 1)
            dve.wait_ge(*filled_at(("BST",)))
            for j in range(2):
                dve.tensor_copy(b_raw[64 * j + R0:64 * j + 2 * R0], psum[ring.bank(("BST",))][0:R0]).then_inc(
                    braw_shared, 1)
            for c in range(KC):
                dve.wait_ge(agt_hi, c + 1)
                minus_hi(ag_s[:, 1, c], psum[ring.bank(("AGT", c))][:, 0:HGW], ag_s[:, 0, c]).then_inc(agt_lo, 1)
            dve.wait_ge(mbt_hi, 1)
            minus_hi(mb_s[:, 1], psum[ring.bank(("MBT",))][:], mb_s[:, 0]).then_inc(mbt_lo, 1)
            dve.wait_ge(gates_done, 1)
            dve.wait_ge(trig_done, 2)
            dve.wait_ge(sin_signed, 1)
            dve.wait_ge(beff_done, GROUPS)
            dve.wait_ge(braw_shared, 2)

            def ln_moments(layer, s, it):
                if layer == 0:
                    dve.wait_ge(x_in[s], 16 * (it + 1))
                else:
                    dve.wait_ge(resid_done, ln_n(layer - 1, s, it))
                dve.bn_stats(stats[:, s % 2], X[:, s]).then_inc(ln_stats, 1)
                dve.wait_ge(ln_stats, ln_n(layer, s, it))
                dve.memset(wait_spot[:], 0.0)
                dve.bn_aggr(mv[:, s % 2], stats[:, s % 2]).then_inc(ln_var, 1)

            def ln_normalize(layer, s, it):
                dve.wait_ge(ln_rstd, ln_n(layer, s, it))
                if s >= 2:
                    dve.wait_ge(*filled_at((f"XT{layer}", s - 2), it))
                elif layer:
                    dve.wait_ge(*filled_at((f"XT{layer - 1}", s + 2), it))
                dve.tensor_scalar(XN[:, s % 2], X[:, s], mv[:, s % 2, 0:1], rstd[:, s % 2], ALU.subtract,
                                  ALU.mult).then_inc(xn_ready, 1)

            def lo_of_transposed(name, it):
                dve.wait_ge(ht_hi, ht_n(name, it))
                side = HT_SIDE[name]
                minus_hi(HT[:, 1, :, side], psum[ring.bank(name)][:].rearrange("p (c t) -> p c t", c=KC),
                         HT[:, 0, :, side]).then_inc(ht_lo, 1)

            def residual(layer, s, it):
                name = (("CTX0", "FFN0", "WO", "BASE")[layer], s)
                dve.wait_ge(*filled_at(name, it))
                y = psum[ring.bank(name)][:]
                if layer == 0:
                    dve.tensor_tensor(X[:, s], y, X[:, s], ALU.add).then_inc(resid_done, 1)
                elif layer == 2:
                    dve.scalar_tensor_tensor(out=X[:, s], in0=y, scalar=tg[:, 1:2], in1=X[:, s], op0=ALU.mult,
                                             op1=ALU.add).then_inc(resid_done, 1)
                elif layer == 1:
                    dve.wait_ge(xb_ready, slot_n(s, it))
                    dve.scalar_tensor_tensor(out=X[:, s], in0=y, scalar=tg[:, 2:3], in1=XB[:, s], op0=ALU.mult,
                                             op1=ALU.add).then_inc(resid_done, 1)
                else:
                    dve.wait_ge(xb3_ready, xb3_n(s, it))
                    dve.scalar_tensor_tensor(out=XB[:, s], in0=y, scalar=tg[:, 3:4], in1=XB[:, s], op0=ALU.mult,
                                             op1=ALU.add).then_inc(resid_done, 1)

            def max0(s, it):
                dve.wait_ge(*filled_at(("SIM", s), it))
                dve.tensor_reduce(smx[:, s, 0:1], psum[ring.bank(("SIM", s))][:, 0:P], AX.X, ALU.max,
                                  negate=True).then_inc(max0_ready, 1)

            def probabilities0(s, it):
                dve.wait_ge(exp0_done, slot_n(s, it))
                recip(smx[:, s, 2:3], smx[:, s, 1:2]).then_inc(sum0_inv, 1)
                dve.wait_ge(sum0_inv, slot_n(s, it))
                dve.tensor_scalar(PR[:, s], PR[:, s], smx[:, s, 2:3], tg[:, 0:1], ALU.mult, ALU.mult).then_inc(
                    p0_ready, 1)

            def a_cat_lo(p, it):
                dve.wait_ge(acat_hi, pair_n(p, it))
                minus_hi(a_cat[:, 1, :, 0::2], a_eff[:, :, bass.ds(it * SLOTS + 2 * p, 2)],
                         a_cat[:, 0, :, 0::2]).then_inc(acat_lo, 1)

            def b_raw_rows(p, it):
                if p:
                    dve.wait_ge(*filled_at(("FFN0", 2 * p - 1), it))
                for j in range(2):
                    r = R0 * (2 * p + j)
                    dve.tensor_copy(b_raw[64 * j:64 * j + R0], b_eff[r:r + R0, bass.ds(it, 1)].squeeze(1)
                                    ).then_inc(braw_ready, 1)

            def b_cat_lo(p, it):
                dve.wait_ge(bcat_hi, pair_n(p, it))
                minus_hi(b_cat[:, 1], b_raw[:], b_cat[:, 0]).then_inc(bcat_lo, 1)

            def axt_lo_part(p, it):
                dve.wait_ge(axt_hi, pair_n(p, it))
                minus_hi(AXT[:, 1], psum[ring.bank(("AX", p))][:, 0:2 * P].rearrange("p (s t) -> p s t", s=2),
                         AXT[:, 0]).then_inc(axt_lo, 1)

            def rotate_products(src, cos_out, sin_out, heads, s, it, done):
                c = rope_cos[:, bass.ds(it * SLOTS + s, 1)].to_broadcast([P, 2 * heads, DH // 2])
                t = rope_sin[:, bass.ds(it * SLOTS + s, 1)].rearrange("p b h d -> p b (h d)").to_broadcast(
                    [P, heads, DH])
                dve.tensor_tensor(cos_out.rearrange("p (h d) -> p h d", d=DH // 2),
                                  src.rearrange("p (h d) -> p h d", d=DH // 2), c, ALU.mult).then_inc(done, 1)
                dve.tensor_tensor(sin_out.rearrange("p (h d) -> p h d", d=DH),
                                  src.rearrange("p (h d) -> p h d", d=DH), t, ALU.mult).then_inc(done, 1)

            def k_products(s, it):
                dve.wait_ge(*filled_at(("KV", s), it))
                if s >= 2:
                    dve.wait_ge(ko_ready, 2 * slot_n(s - 2, it))
                rotate_products(psum[ring.bank(("KV", s))][:, 0:G * DH], KT1[:, s % 2, 0], KT1[:, s % 2, 1], G, s,
                                it, k_prod)

            def q_products(s, it):
                dve.wait_ge(*filled_at(("Q", s), it))
                if s:
                    dve.wait_ge(qo_ready, 2 * slot_n(s - 1, it))
                rotate_products(psum[ring.bank(("Q", s))][:], qr[:, 0], qr[:, 1], H, s, it, q_prod)

            def queries_lo(s, it):
                dve.wait_ge(qn_hi, slot_n(s, it))
                minus_hi(QN[:, 1], psum[ring.bank(("QN", s))][:], QN[:, 0]).then_inc(qn_lo, 1)

            def negative_max(s, it):
                dve.wait_ge(max1_done, it * G * SLOTS + G * (s + 1))
                dve.tensor_copy(NMHL[:, :, 0:G].bitcast(F32R), NM[:]).then_inc(nm_hi, 1)
                dve.wait_ge(nm_hi, slot_n(s, it))
                dve.tensor_tensor(NMHL[:, :, G:2 * G], NM[:], NMHL[:, :, 0:G], ALU.subtract).then_inc(nm_lo, 1)

            def attention_rows(s, half, it):
                name = ("UT", s, half)
                n = it * 2 * SLOTS + (2 * s + half + 1)
                dve.wait_ge(*filled_at(name, it))
                u = psum[ring.bank(name)][:].rearrange("p (r j w) -> p r j w", r=REP, j=REP)
                recip(RS[:, half], u[:, :, :, DH]).then_inc(rs_ready, 1)
                dve.wait_ge(rs_ready, n)
                o = cn[:, half * (D // 2):(half + 1) * (D // 2)].rearrange("p (j r d) -> p r j d", j=REP, r=REP)
                dve.tensor_tensor(o, u[:, :, :, 0:DH], RS[:, half].unsqueeze(3).to_broadcast([P, REP, REP, DH]),
                                  ALU.mult).then_inc(cn_ready, 1)

            with dve.Fori(0, GROUPS, 1) as it:
                ln_moments(0, 0, it)
                ln_moments(0, 1, it)
                ln_normalize(0, 0, it)
                ln_moments(0, 2, it)
                ln_normalize(0, 1, it)
                ln_moments(0, 3, it)
                ln_normalize(0, 2, it)
                max0(0, it)
                ln_normalize(0, 3, it)
                k_products(0, it)
                max0(1, it)
                probabilities0(0, it)
                max0(2, it)
                probabilities0(1, it)
                a_cat_lo(0, it)
                b_raw_rows(0, it)
                max0(3, it)
                probabilities0(2, it)
                probabilities0(3, it)
                for s in range(2):
                    residual(0, s, it)
                    ln_moments(1, s, it)
                ln_normalize(1, 0, it)
                residual(0, 2, it)
                ln_normalize(1, 1, it)
                residual(0, 3, it)
                ln_moments(1, 2, it)
                lo_of_transposed(("XT1", 0), it)
                lo_of_transposed(("XT1", 1), it)
                ln_moments(1, 3, it)
                b_cat_lo(0, it)
                k_products(1, it)
                ln_normalize(1, 2, it)
                axt_lo_part(0, it)
                ln_normalize(1, 3, it)
                k_products(2, it)
                a_cat_lo(1, it)
                residual(1, 0, it)
                ln_moments(2, 0, it)
                lo_of_transposed(("XT1", 2), it)
                b_raw_rows(1, it)
                lo_of_transposed(("XT1", 3), it)
                residual(1, 1, it)
                ln_moments(2, 1, it)
                b_cat_lo(1, it)
                k_products(3, it)
                axt_lo_part(1, it)
                ln_normalize(2, 0, it)
                ln_normalize(2, 1, it)
                residual(1, 2, it)
                ln_moments(2, 2, it)
                lo_of_transposed(("XT2", 0), it)
                residual(1, 3, it)
                ln_moments(2, 3, it)
                lo_of_transposed(("XT2", 1), it)
                ln_normalize(2, 2, it)
                q_products(0, it)
                ln_normalize(2, 3, it)
                queries_lo(0, it)
                lo_of_transposed(("XT2", 2), it)
                q_products(1, it)
                for s in range(SLOTS + 1):
                    if s >= 2:
                        attention_rows(s - 2, 0, it)
                        attention_rows(s - 2, 1, it)
                    if s == 1:
                        lo_of_transposed(("XT2", 3), it)
                    if s >= 3:
                        lo_of_transposed(("XT3", s - 3), it)
                    if s >= 2:
                        lo_of_transposed(("CNT", s - 2), it)
                    if s == SLOTS:
                        residual(2, s - 2, it)
                        ln_moments(3, s - 2, it)
                    if s < SLOTS:
                        for g in range(G):
                            gp, m = g // 2, g % 2
                            if s >= 2 and g == 4:
                                residual(2, s - 2, it)
                                ln_moments(3, s - 2, it)
                            dve.wait_ge(*filled_at(("S1", s, g), it))
                            dve.tensor_reduce(NM[:, 2 * m:2 * m + 2, 2 * gp:2 * gp + 2],
                                              psum[ring.bank(("S1", s, g))][:].rearrange(
                                                  "p (r g t) -> p r g t", r=2, g=2), AX.X, ALU.max,
                                              negate=True).then_inc(max1_done, 1)
                        negative_max(s, it)
                    if s >= 2:
                        ln_normalize(3, s - 2, it)
                    if s + 1 < SLOTS:
                        queries_lo(s + 1, it)
                    if s:
                        dve.wait_ge(*filled_at(("PV", s - 1, 1), it))
                        dve.tensor_copy(CU[:, 1], psum[ring.bank(("PV", s - 1, 1))][:]).then_inc(cu_by_dve, 1)
                    if s + 2 < SLOTS:
                        q_products(s + 2, it)

                count = [0]

                def gate_op(ins):
                    count[0] += 1
                    ins.then_inc(gate_step, 1)
                    dve.wait_ge(gate_step, it * (SLOTS // 2 * GATE_STEPS) + count[0])

                def expert_gates(p):
                    both = slice(2 * p, 2 * p + 2)
                    gates, d, t = hgs[p][:, :, ER:ER + E], gd[:, both], gt[:, both]
                    w, w_norm = gw[:, 0, both], gw[:, 1, both]
                    dve.wait_ge(hg_ready, slot_n(2 * p + 1, it))
                    gate_op(dve.tensor_reduce(d[:, :, 0], gates, AX.X, ALU.max))
                    dve.tensor_tensor(t[:, :, 0:E], gates, d[:, :, 0:1].to_broadcast([P, 2, E]),
                                      ALU.subtract).then_inc(gate_args, 1)
                    dve.tensor_scalar(t[:, :, E], hgs[p][:, :, ER + E], bthr[:], -1.0, ALU.add, ALU.mult).then_inc(
                        gate_args, 1)
                    dve.wait_ge(gate_exp, pair_n(p, it))
                    dve.tensor_scalar(d[:, :, 2], t[:, :, E], 1.0, None, ALU.add).then_inc(one_plus, 1)
                    gate_op(dve.tensor_reduce(d[:, :, 1], t[:, :, 0:E], AX.X, ALU.add))
                    dve.wait_ge(one_plus, pair_n(p, it))
                    gate_op(recip(d[:, :, 3:5], d[:, :, 1:3]))
                    gate_op(dve.tensor_tensor(w, t[:, :, 0:E], d[:, :, 3:4].to_broadcast([P, 2, E]), ALU.mult))
                    gate_op(dve.scalar_tensor_tensor(out=w, in0=d[:, :, 4:5].to_broadcast([P, 2, E]),
                                                     scalar=-1.0 / 8.0, in1=w, op0=ALU.mult, op1=ALU.add))
                    gate_op(dve.tensor_scalar(w, w, 0.0, None, ALU.max))
                    gate_op(dve.tensor_reduce(d[:, :, 5], w, AX.X, ALU.add))
                    gate_op(dve.scalar_tensor_tensor(out=d[:, :, 7], in0=d[:, :, 5], scalar=0.0, in1=d[:, :, 5],
                                                     op0=ALU.is_equal, op1=ALU.add))
                    gate_op(recip(d[:, :, 8], d[:, :, 7]))
                    gate_op(dve.scalar_tensor_tensor(out=w_norm, in0=w, scalar=32.0 / 16.0,
                                                     in1=d[:, :, 8:9].to_broadcast([P, 2, E]), op0=ALU.mult,
                                                     op1=ALU.mult))
                    assert count[0] == (p + 1) * GATE_STEPS
                    for j in range(2):
                        h = hgs[p][:, j, 0:ER].rearrange("p (e r) -> p e r", e=E)
                        dve.tensor_tensor(h, h, w_norm[:, j].unsqueeze(2).to_broadcast([P, E, R1]),
                                          ALU.mult).then_inc(hw_ready, 1)

                def lo_of_experts(s):
                    dve.wait_ge(hwt_hi, slot_n(s, it))
                    minus_hi(HWT[:, s % 2, 1], psum[ring.bank(("HWT", s))][:, 0:P], HWT[:, s % 2, 0]).then_inc(
                        hwt_lo, 1)

                expert_gates(0)
                attention_rows(3, 0, it)
                attention_rows(3, 1, it)
                lo_of_transposed(("XT3", 2), it)
                lo_of_experts(0)
                lo_of_experts(1)
                lo_of_transposed(("CNT", 3), it)
                residual(2, 3, it)
                ln_moments(3, 3, it)
                ln_normalize(3, 3, it)
                lo_of_transposed(("XT3", 3), it)
                residual(3, 0, it)
                residual(3, 1, it)
                expert_gates(1)
                lo_of_experts(2)
                lo_of_experts(3)
                residual(3, 2, it)
                residual(3, 3, it)

        @block.tensor
        def _(pe):
            def wait_each(waits, it):
                first, now = waits(0), waits(it)
                for n, (signal, value) in enumerate(first):
                    others = [(v, m) for m, (sg, v) in enumerate(first) if sg is signal and m != n]
                    if all((value, n) > other for other in others):
                        pe.wait_ge(*now[n])

            def take(name, it=0, data=lambda it: []):
                before = ring.before[name]
                wait_each(lambda it: ([drained(before, it)] if before is not None else []) + data(it), it)
                return psum[ring.bank(name)]

            def transposes(name, pieces, it=0, data=lambda it: []):
                bank, col = take(name, it, data), 0
                for n, piece in enumerate(pieces):
                    k, m = piece.shape[0], piece.shape[1]
                    last = pe.transpose(bank[0:m, col:col + k], piece, ident[0:k, 0:k])
                    col += k
                last.then_inc(filled[ring.bank(name)], 1)

            def split_products(bank_ap, x_hl, w_hl, chunks, first=True, last=True):
                n = 0
                for c in range(chunks):
                    for i, j in ((0, 0), (1, 0), (0, 1)):
                        mm = pe.matmul(bank_ap, x_hl(i, c), w_hl(j, c), start=(first and n == 0),
                                       stop=(last and n == 3 * chunks - 1))
                        n += 1
                return mm

            pe.wait_ge(gate_in, 16)
            pe.wait_ge(spread_made, 1)
            bank = take(("GREP",))
            for k in range(KC):
                mm = pe.matmul(bank[:, k * B:(k + 1) * B], spread_n[0:NL, k], gate_t[0:NL], start=(k == 0),
                               stop=(k == KC - 1), skip_group_check=True)
            mm.then_inc(filled[ring.bank(("GREP",))], 1)
            pe.wait_ge(lora_a_in, 16)
            pe.wait_ge(gsel_made, 1)
            for c in range(KC):
                bank = take(("AEFF", c))
                for k in range(KC):
                    mm = pe.matmul(bank[:, 0:B * R0], lora_a_nat[:, k, c * P:(c + 1) * P],
                                   gsel[:, k].rearrange("p b r -> p (b r)"), start=(k == 0), stop=(k == KC - 1))
                mm.then_inc(filled[ring.bank(("AEFF", c))], 1)
            pe.wait_ge(ident_made, 1)
            pe.wait_ge(lora_b_in, 16 * KC)
            for k in range(KC):
                transposes(("LBT", k), [lora_b_nat[:, c, k * P:(k + 1) * P] for c in range(KC)])
            pe.wait_ge(lbt_done, KC)
            for h in range(GROUPS):
                bank = take(("BEFF", h))
                for k in range(KC):
                    mm = pe.matmul(bank[:], gsel[:, k, h * SLOTS:(h + 1) * SLOTS].rearrange("p b r -> p (b r)"),
                                   lora_b_t[:, k], start=(k == 0), stop=(k == KC - 1))
                mm.then_inc(filled[ring.bank(("BEFF", h))], 1)
            pe.wait_ge(w_base_in, 16)
            for c in range(KC):
                transposes(("WBT", c), [w_base_nat[:, o, c * P:(c + 1) * P] for o in range(KC)])
            pe.wait_ge(small_in, 16 * (5 + KC))
            pe.wait_ge(bs_in, 16)
            transposes(("AST",), [as_nat[0:R0, c * P:(c + 1) * P] for c in range(KC)])
            transposes(("BST",), [bs_nat[:, c] for c in range(KC)])
            for c in range(KC):
                transposes(("AGT", c), [moe_a_nat[:, c * P:(c + 1) * P], gate_nat[0:E + 2, c * P:(c + 1) * P]])
            transposes(("MBT",), [moe_b_nat[:, c * P:(c + 1) * P] for c in range(KC)])
            pe.wait_ge(w_kv_in, 32)
            pe.wait_ge(v1_ready, 1)
            pe.wait_ge(mt_zeroed, 1)
            pe.wait_ge(masks_made, 6)

            def contexts(s, it):
                pe.wait_ge(ctx_in[s], 16 * (it + 1))
                transposes(("CT", s), [C[:, s, c * P:(c + 1) * P] for c in range(KC)], it)

            def normalized(layer, s, it):
                pe.wait_ge(xn_ready, ln_n(layer, s, it))
                transposes((f"XT{layer}", s), [XN[:, s % 2, c * P:(c + 1) * P] for c in range(KC)], it)

            def scores0(s, it):
                bank = take(("SIM", s), it, lambda it: [(ct_ready, slot_n(s, it)), (xt0_ready, slot_n(s, it))])
                for c in range(KC):
                    mm = pe.matmul(bank[:, 0:P], xt0[:, s % 2, c], ct[:, s, c], start=(c == 0), stop=(c == KC - 1))
                mm.then_inc(filled[ring.bank(("SIM", s))], 1)

            def context0(s, it):
                pe.wait_ge(p0_ready, slot_n(s, it))
                pe.matmul(take(("CTX0", s), it)[:], PR[:, s], C[:, s], start=True, stop=True).then_inc(
                    filled[ring.bank(("CTX0", s))], 1)

            def keys_values(s, it):
                bank = take(("KV", s), it, lambda it: [(ct_ready, slot_n(s, it))])
                for c in range(KC):
                    mm = pe.matmul(bank[:, 0:2 * P], ct[:, s, c], wkv[:, c], start=(c == 0), stop=(c == KC - 1))
                mm.then_inc(filled[ring.bank(("KV", s))], 1)

            def lora_down(p, it):
                pe.wait_ge(acat_lo, pair_n(p, it))
                pe.wait_ge(ht_lo, ht_n(("XT1", 2 * p + 1), it))
                bank = take(("AX", p), it)
                split_products(bank[:, 0:2 * P], lambda i, c: a_cat[:, i, c].rearrange("p b r -> p (b r)"),
                               lambda j, c: HT[:, j, c].rearrange("p s t -> p (s t)"), KC).then_inc(
                    filled[ring.bank(("AX", p))], 1)

            def ffn0(s, it):
                pe.wait_ge(w0_lo, 2)
                bank, half = take(("FFN0", s), it), slice(64 * (s % 2), 64 * (s % 2) + 64)
                split_products(bank[:], lambda i, c: HT[:, i, c, s % 2], lambda j, c: w0_s[:, j, c], KC, last=False)
                pe.wait_ge(axt_lo, pair_n(s // 2, it))
                pe.wait_ge(bcat_lo, pair_n(s // 2, it))
                split_products(bank[:], lambda i, c: AXT[half, i, s % 2], lambda j, c: b_cat[half, j], 1,
                               first=False).then_inc(filled[ring.bank(("FFN0", s))], 1)

            def queries(s, it):
                side = HT_SIDE[("XT2", s)]
                pe.wait_ge(wq_lo, 1)
                bank = take(("Q", s), it, lambda it: [(ht_lo, ht_n(("XT2", s), it))])
                split_products(bank[:], lambda i, c: HT[:, i, c, side], lambda j, c: wq_s[:, j, c], KC).then_inc(
                    filled[ring.bank(("Q", s))], 1)

            def keys_on_rows(s, it):
                pe.wait_ge(ks_lo, slot_n(s, it))
                transposes(("KT", s), [KS[:, gp].rearrange("p a b n -> p (a b n)") for gp in range(G // 2)], it)

            def queries_to_rows(s, it):
                pe.wait_ge(qo_ready, 2 * slot_n(s, it))
                transposes(("QN", s), [QO[:, r * P:(r + 1) * P] for r in range(REP)], it)

            def queries_on_rows(s, gp, it):
                bank = take(("QT", s, gp), it, lambda it: [(qn_lo, slot_n(s, it))])
                sel = sel_q[:, gp].rearrange("p b n -> p (b n)")
                pe.matmul(bank[:], sel[:, 0:P], QN[:, 0], start=True, stop=False)
                pe.matmul(bank[:], sel[:, 64:64 + P], QN[:, 1], start=False, stop=True).then_inc(
                    filled[ring.bank(("QT", s, gp))], 1)

            def scores_for_max(s, g, it):
                gp, m = g // 2, g % 2
                bank = take(("S1", s, g), it, lambda it: [(kbd_ready, 2 * slot_n(s, it)), drained(("QT", s, gp), it)])
                for r in range(2):
                    col = (2 * m + r) * P
                    mm = pe.matmul(bank[:, r * 2 * P:(r + 1) * 2 * P], QT[:, s % 2, gp, col:col + P],
                                   KBD[:, s % 2, gp].rearrange("p g t -> p (g t)"), start=(r == 0), stop=(r == 1),
                                   skip_group_check=True)
                mm.then_inc(filled[ring.bank(("S1", s, g))], 1)

            def max_on_rows(s, it):
                pe.wait_ge(nm_lo, slot_n(s, it))
                bank = take(("MT", s), it)
                for r in range(REP):
                    mm = pe.transpose(bank[0:2 * G, r * P:(r + 1) * P], NMHL[:, r], ident[:])
                mm.then_inc(filled[ring.bank(("MT", s))], 1)

            def scores_less_max(s, g, it):
                bank = take(("S2", s, g), it, lambda it: [(mt_ready, slot_n(s, it))])
                pe.matmul(bank[:], KBD[:, s % 2, g // 2, g % 2], QT[:, s % 2, g // 2], start=True, stop=False)
                pe.matmul(bank[:], pick_g[:, g:g + 1].to_broadcast([P, P]), MT[:], start=False, stop=True).then_inc(
                    filled[ring.bank(("S2", s, g))], 1)

            def values(s, half, it):
                bank = take(("PV", s, half), it, lambda it: [
                    (v_ready, slot_n(s, it)), (exp1_done, it * G * SLOTS + (G * s + 4 * (half + 1)))])
                for j in range(4):
                    g = 4 * half + j
                    mm = pe.matmul(bank[32 * j:32 * j + 32], V1[:, s, g], PT[:, g], start=True, stop=True)
                mm.then_inc(filled[ring.bank(("PV", s, half))], 1)

            def values_to_tokens(s, half, it):
                transposes(("UT", s, half), [CU[:, half, r * P:(r + 1) * P] for r in range(REP)], it,
                           lambda it: [(cu_by_dve if half else cu_by_act, slot_n(s, it))])

            def outputs_on_rows(s, it):
                pe.wait_ge(cn_ready, 2 * slot_n(s, it))
                transposes(("CNT", s), [cn[:, c * P:(c + 1) * P] for c in range(KC)], it)

            def attention_out(s, it):
                bank = take(("WO", s), it, lambda it: [(ht_lo, ht_n(("CNT", s), it))])
                side = HT_SIDE[("CNT", s)]
                pe.wait_ge(wo_lo, 1)
                split_products(bank[:], lambda i, c: HT[:, i, c, side], lambda j, c: wo_s[:, j, c], KC).then_inc(
                    filled[ring.bank(("WO", s))], 1)

            def experts_down(s, it):
                side = HT_SIDE[("XT3", s)]
                pe.wait_ge(agt_lo, KC)
                bank = take(("HG", s), it, lambda it: [(ht_lo, ht_n(("XT3", s), it))])
                split_products(bank[:, 0:HGW], lambda i, c: HT[:, i, c, side], lambda j, c: ag_s[:, j, c],
                               KC).then_inc(filled[ring.bank(("HG", s))], 1)

            def base(s, it):
                side = HT_SIDE[("XT3", s)]
                pe.wait_ge(wb_lo, KC)
                split_products(take(("BASE", s), it)[:], lambda i, c: HT[:, i, c, side], lambda j, c: wb_s[:, j, c],
                               KC, last=False)

            def experts_on_rows(s, it):
                pe.wait_ge(hw_ready, slot_n(s, it))
                transposes(("HWT", s), [hgs[s // 2][:, s % 2, 0:ER]], it)

            def experts_up(s, it):
                pe.wait_ge(mbt_lo, 1)
                pe.wait_ge(hwt_lo, slot_n(s, it))
                split_products(psum[ring.bank(("BASE", s))][:], lambda i, c: HWT[:, s % 2, i], lambda j, c: mb_s[:, j],
                               1, first=False).then_inc(filled[ring.bank(("BASE", s))], 1)

            with pe.Fori(0, GROUPS, 1) as it:
                for s in range(SLOTS):
                    contexts(s, it)
                normalized(0, 0, it)
                normalized(0, 1, it)
                keys_values(0, it)
                scores0(0, it)
                normalized(0, 2, it)
                scores0(1, it)
                normalized(0, 3, it)
                scores0(2, it)
                scores0(3, it)
                context0(0, it)
                context0(1, it)
                keys_values(1, it)
                context0(2, it)
                context0(3, it)
                normalized(1, 0, it)
                normalized(1, 1, it)
                keys_values(2, it)
                lora_down(0, it)
                ffn0(0, it)
                normalized(1, 2, it)
                ffn0(1, it)
                normalized(1, 3, it)
                keys_values(3, it)
                lora_down(1, it)
                ffn0(2, it)
                normalized(2, 0, it)
                ffn0(3, it)
                normalized(2, 1, it)
                queries(0, it)
                keys_on_rows(0, it)
                queries(1, it)
                queries_to_rows(0, it)
                normalized(2, 2, it)
                for s in range(SLOTS + 1):
                    if s:
                        max_on_rows(s - 1, it)
                    if s == 1:
                        normalized(2, 3, it)
                    if s >= 3:
                        normalized(3, s - 3, it)
                    if s >= 2:
                        values_to_tokens(s - 2, 0, it)
                        values_to_tokens(s - 2, 1, it)
                    if s < SLOTS:
                        for gp in range(G // 2):
                            queries_on_rows(s, gp, it)
                    if 2 <= s < SLOTS:
                        outputs_on_rows(s - 2, it)
                    for g in range(G):
                        if s:
                            scores_less_max(s - 1, g, it)
                        if s < SLOTS:
                            scores_for_max(s, g, it)
                        if s == SLOTS and g == 1:
                            outputs_on_rows(s - 2, it)
                        if s >= 2 and g == (5 if s == SLOTS else 2):
                            attention_out(s - 2, it)
                        if s and g == 5:
                            values(s - 1, 0, it)
                    if s + 2 < SLOTS:
                        queries(s + 2, it)
                    if s == 3:
                        experts_down(0, it)
                        base(0, it)
                    if s + 1 < SLOTS:
                        keys_on_rows(s + 1, it)
                        queries_to_rows(s + 1, it)
                    if s == SLOTS:
                        experts_down(1, it)
                    if s:
                        values(s - 1, 1, it)
                normalized(3, 2, it)
                values_to_tokens(3, 0, it)
                values_to_tokens(3, 1, it)
                base(1, it)
                experts_on_rows(0, it)
                experts_on_rows(1, it)
                outputs_on_rows(3, it)
                experts_down(2, it)
                attention_out(3, it)
                base(2, it)
                normalized(3, 3, it)
                experts_up(0, it)
                experts_up(1, it)
                experts_down(3, it)
                base(3, it)
                experts_on_rows(2, it)
                experts_on_rows(3, it)
                experts_up(2, it)
                experts_up(3, it)
                wait_each(lambda it: [drained(name, it) for name in ring.end_of_loop], it)


_INS = ["x", "ctx_4096", "itok_BxS2_0_2047", "g_xattn", "g_ffn", "L0_ffn_gate", "L0_ffn_kernel", "L0_ffn_bias",
        "L0_ffn_lora_A", "L0_ffn_lora_B", "L0_ffn_lora_A_shared", "L0_ffn_lora_B_shared", "L1_xattn_Wq",
        "L1_xattn_Wk", "L1_xattn_Wv", "L1_xattn_Wo", "L1_ffn_W_base", "L1_ffn_b_base", "L1_ffn_W_gate",
        "L1_ffn_W_thr", "L1_ffn_b_thr", "L1_ffn_A", "L1_ffn_B"]


def kernel(**inputs):
    import concourse.bacc as bacc
    from concourse.bass_utils import run_bass_kernel_spmd

    nc = bacc.Bacc("TRN2", target_bir_lowering=False, num_devices=1)
    arrays, args = {}, []
    for name in _INS:
        a = np.ascontiguousarray(inputs[name])
        arrays[f"in_{name}"] = a
        args.append(nc.dram_tensor(f"in_{name}", a.shape, mybir.dt.from_np(a.dtype), kind="ExternalInput").ap())
    args.append(nc.dram_tensor("out_0", (B, P, D), F32, kind="ExternalOutput").ap())
    build(nc, *args)
    r = run_bass_kernel_spmd(nc, [arrays], core_ids=[0])
    return r.results[0]["out_0"]
```
